# Optimizing a Trainium2 kernel written in Bass

```python
import numpy as np
import jax
import jax.numpy as jnp

def _softmax(x, axis=-1):
    return jax.nn.softmax(x, axis=axis)

def _gelu(x):
    return jax.nn.gelu(x, approximate=True)

def _silu(x):
    return jax.nn.silu(x)

def _sigmoid(x):
    return jax.nn.sigmoid(x)

def _layernorm(x, axis=-1, eps=1e-05):
    m = jnp.mean(x, axis=axis, keepdims=True)
    v = jnp.var(x, axis=axis, keepdims=True)
    return (x - m) / jnp.sqrt(v + eps)

def _scatter_add(tgt, idx, src, axis=0):
    return tgt.at[idx].add(src)

def _segment_sum(src, seg, n):
    return jax.ops.segment_sum(src, seg, n)
kernel_name = 'mk_audio_tower_d1_tok_audfeat512_r4_ba0586'

def setup_inputs(seed: int=0):
    np.random.seed(seed)
    _w = jnp.asarray

    def _rec_inputs():
        import jax
        import jax.numpy as jnp
        _rk = jax.random.key(seed)
        x = -0.00056805 + 1.00052 * jax.random.normal(jax.random.fold_in(_rk, 1), (16, 8008, 1), jnp.float32)
        return x
    x = _rec_inputs()

    def _L0_tok_setup():
        import jax, jax.numpy as jnp
        import numpy as np
        PATCH_LEN = 64
        STRIDE = 32
        D_MODEL = 128
        key = jax.random.key(seed)
        k1, k2, k3 = jax.random.split(key, 3)
        x = jax.random.normal(k1, (64, 8008, 1), dtype=jnp.float32)
        W = jax.random.normal(k2, (D_MODEL, PATCH_LEN), dtype=jnp.float32) * 0.05
        pos_embed = jax.random.normal(k3, (1, 250, D_MODEL), dtype=jnp.float32)
        return {'x': x, 'W': W, 'pos_embed': pos_embed}
    _L0_tok_all = _L0_tok_setup()
    _L0_tok_in = {k: v for k, v in _L0_tok_all.items() if k in ('W', 'pos_embed')}
    del _L0_tok_all

    def _L0_attn_setup():
        import jax, jax.numpy as jnp
        import numpy as np
        B, L, D, N, OUT, NL = (4, 256, 128, 16, 128, 2)

        def _linear_scan(a, b):

            def comb(c1, c2):
                a1, b1 = c1
                a2, b2 = c2
                return (a1 * a2, a2 * b1 + b2)
            return jax.lax.associative_scan(comb, (a, b), axis=1)[1]

        def _forward(x, A, D_skip, WB, bB, WC, bC, Wdt, bdt, Wlin, blin, Wdec, bdec):
            y = x
            for i in range(NL):
                dt = jax.nn.softplus(jnp.einsum('bld,de->ble', y, Wdt[i]) + bdt[i])
                Bm = jnp.einsum('bld,dn->bln', y, WB[i]) + bB[i]
                Cm = jnp.einsum('bld,dn->bln', y, WC[i]) + bC[i]
                a = jnp.exp(dt[..., None] * A[i])
                b = (dt * y)[..., None] * Bm[:, :, None, :]
                h = _linear_scan(a, b)
                out = jnp.einsum('bldn,bln->bld', h, Cm) + D_skip[i] * y
                y = jnp.maximum(out, 0.0)
                y = jnp.einsum('bld,de->ble', y, Wlin[i]) + blin[i]
            return jnp.einsum('bld,do->blo', y, Wdec) + bdec
        key = jax.random.key(seed)
        ks = jax.random.split(key, 8)
        sc = D ** (-0.5)
        return {'x': jax.random.normal(ks[0], (B, L, D), jnp.float32), 'A': -jax.random.uniform(ks[1], (NL, D, N), jnp.float32, 0.1, 1.0), 'D_skip': jnp.ones((NL, D), jnp.float32), 'WB': jax.random.normal(ks[2], (NL, D, N), jnp.float32) * sc, 'bB': jnp.zeros((NL, N), jnp.float32), 'WC': jax.random.normal(ks[3], (NL, D, N), jnp.float32) * sc, 'bC': jnp.zeros((NL, N), jnp.float32), 'Wdt': jax.random.normal(ks[4], (NL, D, D), jnp.float32) * sc, 'bdt': jnp.full((NL, D), -4.0, jnp.float32), 'Wlin': jax.random.normal(ks[5], (NL, D, D), jnp.float32) * sc, 'blin': jnp.zeros((NL, D), jnp.float32), 'Wdec': jax.random.normal(ks[6], (D, OUT), jnp.float32) * sc, 'bdec': jnp.zeros((OUT,), jnp.float32)}
    _L0_attn_all = _L0_attn_setup()
    _L0_attn_in = {k: v for k, v in _L0_attn_all.items() if k in ('A', 'D_skip', 'WB', 'bB', 'WC', 'bC', 'Wdt', 'bdt', 'Wlin', 'blin', 'Wdec', 'bdec')}
    del _L0_attn_all

    def _L0_ffn_setup():
        import jax, jax.numpy as jnp
        import numpy as np
        B, T, D, F, E, K = (8, 256, 128, 512, 8, 2)

        def _moe_forward(x, Wr, br, W1, b1, W2, b2):
            Bx, Tx, Dx = x.shape
            xf = x.reshape(-1, Dx)
            logits = xf @ Wr + br
            probs = jax.nn.softmax(logits, axis=-1)
            vals, idx = jax.lax.top_k(probs, K)
            cw = (jax.nn.one_hot(idx, E, dtype=x.dtype) * vals[..., None]).sum(axis=1)

            def body(acc, params):
                W1e, b1e, W2e, b2e, cwe = params
                h = jax.nn.relu(xf @ W1e + b1e)
                y = h @ W2e + b2e
                return (acc + cwe[:, None] * y, None)
            out, _ = jax.lax.scan(body, jnp.zeros_like(xf), (W1, b1, W2, b2, cw.T))
            return out.reshape(Bx, Tx, Dx)
        key = jax.random.key(seed)
        k0, k1, k2, k3 = jax.random.split(key, 4)
        s_d = 1.0 / np.sqrt(D)
        s_f = 1.0 / np.sqrt(F)
        return {'x': jax.random.normal(k0, (B, T, D), jnp.float32), 'Wr': jax.random.uniform(k1, (D, E), jnp.float32, -s_d, s_d), 'br': jnp.zeros((E,), jnp.float32), 'W1': jax.random.uniform(k2, (E, D, F), jnp.float32, -s_d, s_d), 'b1': jnp.zeros((E, F), jnp.float32), 'W2': jax.random.uniform(k3, (E, F, D), jnp.float32, -s_f, s_f), 'b2': jnp.zeros((E, D), jnp.float32)}
    _L0_ffn_all = _L0_ffn_setup()
    _L0_ffn_in = {k: v for k, v in _L0_ffn_all.items() if k in ('Wr', 'br', 'W1', 'b1', 'W2', 'b2')}
    del _L0_ffn_all
    return {'x': x, 'L0_tok_W': _L0_tok_in['W'], 'L0_tok_pos_embed': _L0_tok_in['pos_embed'], 'L0_attn_A': _L0_attn_in['A'], 'L0_attn_D_skip': _L0_attn_in['D_skip'], 'L0_attn_WB': _L0_attn_in['WB'], 'L0_attn_bB': _L0_attn_in['bB'], 'L0_attn_WC': _L0_attn_in['WC'], 'L0_attn_bC': _L0_attn_in['bC'], 'L0_attn_Wdt': _L0_attn_in['Wdt'], 'L0_attn_bdt': _L0_attn_in['bdt'], 'L0_attn_Wlin': _L0_attn_in['Wlin'], 'L0_attn_blin': _L0_attn_in['blin'], 'L0_attn_Wdec': _L0_attn_in['Wdec'], 'L0_attn_bdec': _L0_attn_in['bdec'], 'L0_ffn_Wr': _L0_ffn_in['Wr'], 'L0_ffn_br': _L0_ffn_in['br'], 'L0_ffn_W1': _L0_ffn_in['W1'], 'L0_ffn_b1': _L0_ffn_in['b1'], 'L0_ffn_W2': _L0_ffn_in['W2'], 'L0_ffn_b2': _L0_ffn_in['b2']}

def reference(x, L0_tok_W, L0_tok_pos_embed, L0_attn_A, L0_attn_D_skip, L0_attn_WB, L0_attn_bB, L0_attn_WC, L0_attn_bC, L0_attn_Wdt, L0_attn_bdt, L0_attn_Wlin, L0_attn_blin, L0_attn_Wdec, L0_attn_bdec, L0_ffn_Wr, L0_ffn_br, L0_ffn_W1, L0_ffn_b1, L0_ffn_W2, L0_ffn_b2):
    import jax
    import jax.numpy as jnp

    def _L0_tok_ref(x, W, pos_embed):
        import jax, jax.numpy as jnp
        import numpy as np
        PATCH_LEN = 64
        STRIDE = 32
        D_MODEL = 128
        B, L, _ = x.shape
        num_patches = (L - PATCH_LEN) // STRIDE + 1
        idx = jnp.arange(num_patches)[:, None] * STRIDE + jnp.arange(PATCH_LEN)[None, :]
        patches = x[:, idx, 0]
        out = jnp.einsum('bnp,dp->bnd', patches, W)
        return out + pos_embed[:, :num_patches, :]

    def _L0_attn_ref(x, A, D_skip, WB, bB, WC, bC, Wdt, bdt, Wlin, blin, Wdec, bdec):
        import jax, jax.numpy as jnp
        import numpy as np
        B, L, D, N, OUT, NL = (4, 256, 128, 16, 128, 2)

        def _linear_scan(a, b):

            def comb(c1, c2):
                a1, b1 = c1
                a2, b2 = c2
                return (a1 * a2, a2 * b1 + b2)
            return jax.lax.associative_scan(comb, (a, b), axis=1)[1]

        def _forward(x, A, D_skip, WB, bB, WC, bC, Wdt, bdt, Wlin, blin, Wdec, bdec):
            y = x
            for i in range(NL):
                dt = jax.nn.softplus(jnp.einsum('bld,de->ble', y, Wdt[i]) + bdt[i])
                Bm = jnp.einsum('bld,dn->bln', y, WB[i]) + bB[i]
                Cm = jnp.einsum('bld,dn->bln', y, WC[i]) + bC[i]
                a = jnp.exp(dt[..., None] * A[i])
                b = (dt * y)[..., None] * Bm[:, :, None, :]
                h = _linear_scan(a, b)
                out = jnp.einsum('bldn,bln->bld', h, Cm) + D_skip[i] * y
                y = jnp.maximum(out, 0.0)
                y = jnp.einsum('bld,de->ble', y, Wlin[i]) + blin[i]
            return jnp.einsum('bld,do->blo', y, Wdec) + bdec
        return _forward(x, A, D_skip, WB, bB, WC, bC, Wdt, bdt, Wlin, blin, Wdec, bdec)

    def _L0_ffn_ref(x, Wr, br, W1, b1, W2, b2):
        import jax, jax.numpy as jnp
        import numpy as np
        B, T, D, F, E, K = (8, 256, 128, 512, 8, 2)

        def _moe_forward(x, Wr, br, W1, b1, W2, b2):
            Bx, Tx, Dx = x.shape
            xf = x.reshape(-1, Dx)
            logits = xf @ Wr + br
            probs = jax.nn.softmax(logits, axis=-1)
            vals, idx = jax.lax.top_k(probs, K)
            cw = (jax.nn.one_hot(idx, E, dtype=x.dtype) * vals[..., None]).sum(axis=1)

            def body(acc, params):
                W1e, b1e, W2e, b2e, cwe = params
                h = jax.nn.relu(xf @ W1e + b1e)
                y = h @ W2e + b2e
                return (acc + cwe[:, None] * y, None)
            out, _ = jax.lax.scan(body, jnp.zeros_like(xf), (W1, b1, W2, b2, cw.T))
            return out.reshape(Bx, Tx, Dx)
        return _moe_forward(x, Wr, br, W1, b1, W2, b2)
    h = _L0_tok_ref(x, L0_tok_W, L0_tok_pos_embed)
    h = h + _L0_attn_ref(_layernorm(h, axis=-1), L0_attn_A, L0_attn_D_skip, L0_attn_WB, L0_attn_bB, L0_attn_WC, L0_attn_bC, L0_attn_Wdt, L0_attn_bdt, L0_attn_Wlin, L0_attn_blin, L0_attn_Wdec, L0_attn_bdec)
    h = h + _L0_ffn_ref(_layernorm(h, axis=-1), L0_ffn_Wr, L0_ffn_br, L0_ffn_W1, L0_ffn_b1, L0_ffn_W2, L0_ffn_b2)
    return h

_drawn_inputs = setup_inputs


def setup_inputs(seed=0):
    import zlib

    import numpy as np

    out = dict(_drawn_inputs(seed))
    spreads = {'L0_attn_D_skip': (1.0, 0.2),
     'L0_attn_bB': (0.0, 0.1),
     'L0_attn_bC': (0.0, 0.1),
     'L0_attn_bdt': (-4.0, 0.2),
     'L0_attn_blin': (0.0, 0.1),
     'L0_attn_bdec': (0.0, 0.392),
     'L0_ffn_br': (0.0, 0.8),
     'L0_ffn_b1': (0.0, 0.8),
     'L0_ffn_b2': (0.0, 0.8)}
    factors = {'L0_ffn_Wr': 4.015, 'L0_ffn_W1': 4.537, 'L0_ffn_W2': 3.727}
    for name, (base, spread) in spreads.items():
        noise = np.random.default_rng([zlib.crc32(name.encode()), seed]).standard_normal(out[name].shape)
        drawn = base * np.exp(spread * noise) if base else spread * noise
        out[name] = jnp.asarray(drawn.astype(out[name].dtype))
    for name, factor in factors.items():
        out[name] = (out[name] * factor).astype(out[name].dtype)
    return out
```

```python
import numpy as np
import concourse.bass as bass
from concourse import mybir
from contextlib import ExitStack

SEQS, LENGTH, CHANNELS, STATES, LAYERS = 16, 249, 128, 16, 2
PATCH, STRIDE = 64, 32
EXPERTS, HIDDEN, TOP = 8, 512, 2
PER_TILE = 2
TOK = PER_TILE * LENGTH
TILES = SEQS // PER_TILE
TOKENS = SEQS * LENGTH
GROUPS = CHANNELS // (128 // STATES)
GCH = CHANNELS // GROUPS
BANK = 512
CHUNK = 125
CHUNK_AT = [0, 125, 249, 373]
FCH = HIDDEN // 128
EPS = 1e-5


def audio_tower(nc, x_rows, w_tok, pos, a_cols, w_dt, w_b, w_c, w_lin, w_dec, vecs, w_r, b_r, w_1, b_1, w_2, b_2,
                spread, gather, eye, earlier, out):
    f32, f32r = mybir.dt.float32, mybir.dt.float32r
    ALU, ACT, AX = mybir.AluOpType, mybir.ActivationFunctionType, mybir.AxisListType

    with ExitStack() as ctx:
        def sb(name, shape, dt=f32):
            return ctx.enter_context(nc.sbuf_tensor(name, shape, dt))

        def sem(name):
            return ctx.enter_context(nc.semaphore(name))

        rows = sb("rows", [PATCH, SEQS, LENGTH])
        wtok = sb("wtok", [PATCH, CHANNELS])
        pos2 = sb("pos2", [128, PER_TILE, LENGTH])
        acol = sb("acol", [128, LAYERS, GROUPS])
        wdt = sb("wdt", [128, LAYERS, 128])
        wb16 = sb("wb16", [128, LAYERS, STATES])
        wc16 = sb("wc16", [128, LAYERS, STATES])
        wb = sb("wb", [128, LAYERS, STATES, GCH])
        wc = sb("wc", [128, LAYERS, STATES, GCH])
        wlin = sb("wlin", [128, LAYERS, 128])
        wdec = sb("wdec", [128, 128])
        NV = 14
        vec = sb("vec", [128, NV])
        bdt, bbr, bcr, dsk, bln = (lambda l, k=k: vec[:, 2 * k + l:2 * k + l + 1] for k in range(5))
        bdec, epsc, zero, one = (vec[:, 10 + k:11 + k] for k in range(4))
        spread_in = sb("spread_in", [128, 8, 128])
        spreadr = sb("spreadr", [128, 8, 128], f32r)
        gath = sb("gath", [128, 4, 32])
        mean_w = sb("mean_w", [128, 128])
        ident = sb("ident", [128, 128])
        earl = sb("earl", [128, EXPERTS, EXPERTS])
        wr = sb("wr", [128, EXPERTS])
        brr = sb("brr", [128, EXPERTS])
        w1 = sb("w1", [128, EXPERTS, HIDDEN])
        b1 = sb("b1", [128, EXPERTS, FCH])
        w2 = sb("w2", [128, EXPERTS, FCH, 128])
        b2 = sb("b2", [EXPERTS, 128])

        hT = sb("hT", [128, TILES * TOK])
        Y = [[sb(f"Y{p}{l}", [128, TOK]) for l in range(LAYERS)] for p in range(2)]
        B = [sb(f"B{p}", [128, TOK]) for p in range(2)]
        C = [sb(f"C{p}", [128, TOK]) for p in range(2)]
        S_dt = [sb(f"S_dt{p}", [128, 2, TOK], f32r) for p in range(2)]
        S_dx = [sb(f"S_dx{p}", [128, 2, TOK], f32r) for p in range(2)]
        decay = [sb(f"decay{k}", [128, PER_TILE, LENGTH]) for k in range(4)]
        state = [sb(f"state{k}", [128, TOK]) for k in range(4)]
        hc = [sb(f"hc{k}", [128, TOK]) for k in range(8)]
        skip = sb("skip", [128, TOK])
        act_y = sb("act_y", [128, TOK])
        lin1 = sb("lin1", [128, TOK])
        zpre = sb("zpre", [128, TOK])
        zexp = sb("zexp", [128, TOK])
        dt = sb("dt", [128, TOK])
        dx = sb("dx", [128, TOK])
        dt_hi, dt_lo, dx_hi, dx_lo = (sb(n, [128, TOK], f32r) for n in ("dt_hi", "dt_lo", "dx_hi", "dx_lo"))
        cen = sb("cen", [128, TOK])
        sq = sb("sq", [128, TOK])
        rstd = sb("rstd", [128, TOK])
        xn = sb("xn", [128, TOK])
        cen_h = sb("cen_h", [128, TOK])
        hid = [[sb(f"hid{k}{c}", [128, TOK]) for c in range(FCH)] for k in range(2)]
        prob = sb("prob", [CHUNK, 4, EXPERTS])
        lmax = sb("lmax", [CHUNK, 4])
        lsum = sb("lsum", [CHUNK, 4])
        lrec = sb("lrec", [CHUNK, 4])
        gt = sb("gt", [CHUNK, 4, EXPERTS, EXPERTS])
        eq = sb("eq", [CHUNK, 4, EXPERTS, EXPERTS])
        rank = sb("rank", [CHUNK, 4, EXPERTS])
        gate = sb("gate", [CHUNK, 4, EXPERTS])
        gateT = sb("gateT", [EXPERTS, 4, CHUNK])
        acc = sb("acc", [CHUNK, 4, 128])

        psum = ctx.enter_context(nc.psum_tensor("psum", [128, 8 * BANK], f32))

        def bank(k, n=TOK, p=128):
            return psum[0:p, k * BANK:k * BANK + n]

        DT, DX, NSUM, POST, PRE = 0, 2, 5, 6, 7

        param_in, tok_in, moe_in = sem("param_in"), sem("tok_in"), sem("moe_in")
        consts = sem("consts")
        rep_dt, rep_dx = sem("rep_dt"), sem("rep_dx")
        exp_done, b_done, scan_done = sem("exp_done"), sem("b_done"), sem("scan_done")
        hc_done, nsum_done = sem("hc_done"), sem("nsum_done")
        skip_done, relu_done, lin_done, linb_done = sem("skip_done"), sem("relu_done"), sem("lin_done"), sem("linb_done")
        dec_done, resid_done = sem("dec_done"), sem("resid_done")
        tok_done, h_done, mean_done, cen_done = sem("tok_done"), sem("h_done"), sem("mean_done"), sem("cen_done")
        sq_done, var_done, ln_done, rstd_done, y0_done = (sem(n) for n in ("sq_done", "var_done", "ln_done", "rstd_done", "y0_done"))
        wdt_done, z_done, soft_done, dt_done, dx_done = (sem(n) for n in ("wdt_done", "z_done", "soft_done", "dt_done", "dx_done"))
        hi_done, dtlo_done, dxlo_done, s_in = sem("hi_done"), sem("dtlo_done"), sem("dxlo_done"), sem("s_in")
        wb_done, b_ready, wc_done, c_ready = (sem(n) for n in ("wb_done", "b_ready", "wc_done", "c_ready"))

        m_h = sem("m_h")
        m_mean, m_cen, m_sq, m_var, m_ln, m_rstd, m_xn = (sem("m_" + n) for n in ("mean", "cen", "sq", "var", "ln", "rstd", "xn"))
        logit_done, shift_done, pexp_done, gate_step, gate_done = (sem(n) for n in ("logit_done", "shift_done", "pexp_done", "gate_step", "gate_done"))
        gateT_done, gateT_ready, init_done, init_ready = (sem(n) for n in ("gateT_done", "gateT_ready", "init_done", "init_ready"))
        up_done, hid_done, down_done, comb_done, out_done = (sem(n) for n in ("up_done", "hid_done", "down_done", "comb_done", "out_done"))

        block = ctx.enter_context(nc.Block())

        def run_slots(engine, slot):
            slot(0, 0)
            with engine.Fori(0, TILES // 2 - 1) as q:
                for c in (1, 2, 3):
                    slot(q, c)
                slot(q + 1, 0)
            for c in (1, 2, 3):
                slot(TILES // 2 - 1, c)

        def starts(q):
            return isinstance(q, int) and q == 0

        def group(i):
            return (i % 4) * 4 + i // 4

        def posted_tile(q, c):
            return 2 * q - 1 if c == 0 else 2 * q

        def prepared_tile(q, c):
            return 2 * q + 1 if c == 0 else 2 * q + 2

        def last(q, c):
            return isinstance(q, int) and q == TILES // 2 - 1 and c == 3

        def tile_of(tensor, t):
            return tensor[:, bass.ds(t * TOK, TOK)]

        PARAM_DMAS = 17

        @block.sync
        def _(sp):
            for dst, src in ((wtok[:], w_tok), (wdt[:], w_dt), (wb16[:], w_b), (wc16[:], w_c), (vec[:], vecs),
                             (acol[:], a_cols), (pos2[:, 0, :], pos), (pos2[:, 1, :], pos), (spread_in[:], spread),
                             (gath[:], gather), (wlin[:], w_lin), (wdec[:], w_dec), (ident[:], eye), (earl[:], earlier),
                             (wr[:], w_r), (brr[:], b_r), (b2[:], b_2)):
                sp.dma_start(dst, src).then_inc(param_in, 16)
            sp.dma_start(w1[:], w_1).then_inc(moe_in, 16)
            sp.dma_start(w2[:], w_2).then_inc(moe_in, 16)
            sp.dma_start(b1[:], b_1).then_inc(moe_in, 16)

            def value(x):
                return x if isinstance(x, int) else sp.snap(x)

            def place_split(x, par):
                first_hi, second_hi, lo_x = value(2 * x + 1), value(2 * x + 2), value(x + 1)
                for n, (S, hi, lo, lo_done) in enumerate(((S_dt, dt_hi, dt_lo, dtlo_done), (S_dx, dx_hi, dx_lo, dxlo_done))):
                    sp.wait_ge(hi_done, (first_hi, second_hi)[n])
                    sp.dma_start(S[par][0:64, 0, :].bitcast(f32), hi[0:64, :].bitcast(f32)).then_inc(s_in, 16)
                    sp.dma_start(S[par][64:128, 1, :].bitcast(f32), hi[64:128, :].bitcast(f32)).then_inc(s_in, 16)
                    sp.wait_ge(lo_done, lo_x)
                    sp.dma_start(S[par][64:128, 0, :].bitcast(f32), lo[0:64, :].bitcast(f32)).then_inc(s_in, 16)
                    sp.dma_start(S[par][0:64, 1, :].bitcast(f32), lo[64:128, :].bitcast(f32)).then_inc(s_in, 16)

            place_split(0, 0)

            def slot(q, c):
                if not last(q, c):
                    place_split(4 * q + c + 1, (c + 1) % 2)

            run_slots(sp, slot)

            with sp.Fori(0, TILES) as t:
                tile_end, row = sp.snap((t + 1) * EXPERTS), sp.snap(t * TOK)
                sp.wait_ge(comb_done, tile_end)
                for k in range(4):
                    skip_rows = int(CHUNK_AT[k] < CHUNK * k)
                    n = CHUNK - skip_rows
                    sp.dma_start(out[bass.ds(row + CHUNK_AT[k] + skip_rows, n), :],
                                 acc[skip_rows:CHUNK, k, :]).then_inc(out_done, 16)
            sp.wait_ge(out_done, TILES * 4 * 16)

        @block.gpsimd
        def _(pool):
            half = LENGTH + 1
            pool.dma_start(rows[0:STRIDE, :, :], x_rows[:, :, 0:LENGTH]).then_inc(tok_in, 16)
            pool.dma_start(rows[STRIDE:PATCH, :, :], x_rows[:, :, 1:half]).then_inc(tok_in, 16)

            def split(x, par, layer):
                y = Y[par][layer]
                pool.wait_ge(dt_done, x + 1)
                if not (isinstance(x, int) and x == 0):
                    pool.wait_ge(s_in, 128 * x)
                    pool.wait_ge(dxlo_done, x)
                nc.gpsimd.tensor_tensor(dx[:], dt[:], y[:], ALU.mult).then_inc(dx_done, 1)
                pool.wait_ge(hi_done, 2 * x + 1)
                nc.gpsimd.tensor_tensor(dt_lo[:], dt[:], dt_hi[:].bitcast(f32), ALU.subtract).then_inc(dtlo_done, 1)

            split(0, 0, 0)

            def slot(q, c):
                s, par = 4 * q + c, c % 2
                layer = c // 2
                nxt = (c + 1) % 4
                for i in range(GROUPS):
                    if i == 0:
                        pool.wait_ge(c_ready, s + 1)
                    pool.wait_ge(scan_done, 16 * s + i + 1)
                    if not (starts(q) and c == 0 and i < 8):
                        pool.wait_ge(nsum_done, 4 * s + i // 4 - 1)
                    nc.gpsimd.tensor_tensor(hc[i % 8][:], state[i % 4][:], C[par][:], ALU.mult).then_inc(hc_done, 1)
                    if i == 11 and not last(q, c):
                        split(s + 1, nxt % 2, nxt // 2)

            run_slots(pool, slot)

        @block.scalar
        def _(act):
            nc.scalar.preload_act_table_set("natural_log_exp_and_others")
            act.wait_ge(param_in, 16 * PARAM_DMAS)

            def softplus(x):
                act.wait_ge(wdt_done, x + 1)
                if not (isinstance(x, int) and x == 0):
                    act.wait_ge(dt_done, x)
                l = None
                nc.scalar.activation(zpre[:], bank(PRE), ACT.Identity, bias=bdt_col[0]).then_inc(z_done, 1)
                act.wait_ge(z_done, x + 1)
                nc.scalar.activation(zexp[:], zpre[:], ACT.Abs).then_inc(soft_done, 1)
                act.wait_ge(soft_done, 3 * x + 1)
                nc.scalar.activation(zexp[:], zexp[:], ACT.Exp, scale=-1.0).then_inc(soft_done, 1)
                act.wait_ge(soft_done, 3 * x + 2)
                nc.scalar.activation(zexp[:], zexp[:], ACT.Ln, bias=one).then_inc(soft_done, 1)

            bdt_col = [None]

            def b_rows(x, par, layer):
                act.wait_ge(wb_done, x + 1)
                if not (isinstance(x, int) and x < 2):
                    act.wait_ge(b_done, 16 * (x - 1))
                nc.scalar.activation(B[par][:], bank(PRE), ACT.Identity, bias=bbr(layer)).then_inc(b_ready, 1)

            def c_rows(x, par, layer):
                act.wait_ge(wc_done, x + 1)
                if not (isinstance(x, int) and x < 2):
                    act.wait_ge(hc_done, 16 * (x - 1))
                nc.scalar.activation(C[par][:], bank(PRE), ACT.Identity, bias=bcr(layer)).then_inc(c_ready, 1)

            def high(x, n):
                act.wait_ge((dt_done, dx_done)[n], x + 1)
                if n == 0 and not (isinstance(x, int) and x == 0):
                    act.wait_ge(s_in, 128 * x)
                if n == 0 and not (isinstance(x, int) and x < 2):
                    act.wait_ge(exp_done, 16 * (x - 1))
                    act.wait_ge(b_done, 16 * (x - 1))
                nc.scalar.copy((dt_hi, dx_hi)[n][:], (dt, dx)[n][:]).then_inc(hi_done, 1)

            def square(t):
                act.wait_ge(cen_done, t + 1)
                nc.scalar.activation(sq[:], cen[:], ACT.Square).then_inc(sq_done, 1)

            def inverse_std(t):
                act.wait_ge(var_done, t + 1)
                nc.scalar.activation(rstd[:], bank(PRE), ACT.Ln, bias=epsc).then_inc(ln_done, 1)
                act.wait_ge(ln_done, t + 1)
                nc.scalar.activation(rstd[:], rstd[:], ACT.Exp, scale=-0.5).then_inc(rstd_done, 1)

            def relu(x):
                act.wait_ge(skip_done, x + 1)
                nc.scalar.activation(act_y[:], skip[:], ACT.Relu).then_inc(relu_done, 1)

            def lin_bias(x, par, layer):
                act.wait_ge(lin_done, x + 1)
                out_ = Y[par][1] if layer == 0 else lin1
                nc.scalar.activation(out_[:], bank(POST), ACT.Identity, bias=bln(layer)).then_inc(linb_done, 1)

            square(0)
            inverse_std(0)
            bdt_col[0] = bdt(0)
            softplus(0)
            b_rows(0, 0, 0)
            c_rows(0, 0, 0)
            high(0, 0)
            high(0, 1)

            def slot(q, c):
                s, par, layer = 4 * q + c, c % 2, c // 2
                nxt, prv = (c + 1) % 4, (c + 3) % 4
                middle = c in (1, 2)
                for i in range(GROUPS):
                    act.wait_ge(rep_dt, 16 * s + i + 1)
                    if not (starts(q) and c == 0 and i < 4):
                        act.wait_ge(scan_done, 16 * s + i - 3)
                    nc.scalar.activation(decay[i % 4][:, :, 1:LENGTH],
                                         bank(DT + i % 2).rearrange("p (b t) -> p b t", b=PER_TILE)[:, :, 1:LENGTH],
                                         ACT.Exp, scale=acol[:, layer, group(i):group(i) + 1]).then_inc(exp_done, 1)
                    if not (starts(q) and c == 0):
                        if i == 4:
                            relu(s - 1)
                        if i == 6:
                            lin_bias(s - 1, prv % 2, prv // 2)
                    if last(q, c):
                        continue
                    if not middle and i == 3:
                        square(prepared_tile(q, c))
                    if not middle and i == 5:
                        inverse_std(prepared_tile(q, c))
                    if i == 8:
                        bdt_col[0] = bdt(nxt // 2)
                        softplus(s + 1)
                    if i == 9:
                        b_rows(s + 1, nxt % 2, nxt // 2)
                    if i == 10:
                        c_rows(s + 1, nxt % 2, nxt // 2)
                    if i == 11:
                        high(s + 1, 0)
                    if i == 12:
                        high(s + 1, 1)

            run_slots(act, slot)
            relu(15)
            lin_bias(15, 1, 1)

            act.wait_ge(moe_in, 48)
            with act.Fori(0, TILES) as t:
                act.wait_ge(m_cen, t + 1)
                nc.scalar.activation(sq[:], cen[:], ACT.Square).then_inc(m_sq, 1)
                act.wait_ge(m_var, t + 1)
                nc.scalar.activation(rstd[:], bank(7), ACT.Ln, bias=epsc).then_inc(m_ln, 1)
                act.wait_ge(m_ln, t + 1)
                nc.scalar.activation(rstd[:], rstd[:], ACT.Exp, scale=-0.5).then_inc(m_rstd, 1)
                act.wait_ge(shift_done, t + 1)
                nc.scalar.activation(prob[:], prob[:], ACT.Exp).then_inc(pexp_done, 1)
                for e in range(EXPERTS):
                    for f in range(FCH):
                        act.wait_ge(up_done, t * 32 + 4 * e + f + 1)
                        if e >= 2:
                            act.wait_ge(down_done, t * EXPERTS + e - 1)
                        nc.scalar.activation(hid[e % 2][f][:], bank(f), ACT.Relu,
                                             bias=b1[:, e, f:f + 1]).then_inc(hid_done, 1)
                    if e == 0:
                        act.wait_ge(gateT_done, t + 1)
                        nc.scalar.copy(gateT[:].rearrange("e k p -> e (k p)"), bank(7, 4 * CHUNK, EXPERTS)).then_inc(gateT_ready, 1)
                        act.wait_ge(init_done, t + 1)
                        nc.scalar.copy(acc[:].rearrange("p k d -> p (k d)"), bank(6, 512, CHUNK)).then_inc(init_ready, 1)
                act.wait_ge(out_done, (t + 1) * 64)

        @block.vector
        def _(dve):
            nc.vector.memset(mean_w[:], 1.0 / CHANNELS).then_inc(consts, 1)
            for k in range(4):
                nc.vector.memset(decay[k][:, :, 0:1], 0.0).then_inc(consts, 1)
            dve.wait_ge(param_in, 16 * PARAM_DMAS)
            nc.vector.tensor_copy(spreadr[:], spread_in[:]).then_inc(consts, 1)
            for l in range(LAYERS):
                for wide, narrow in ((wb, wb16), (wc, wc16)):
                    nc.vector.tensor_copy(wide[:, l, :, :],
                                          narrow[:, l, :].unsqueeze(2).to_broadcast([128, STATES, GCH])).then_inc(consts, 1)
            CONSTS = 1 + 4 + 1 + 2 * LAYERS

            def embed(t):
                dve.wait_ge(tok_done, t + 1)
                nc.vector.tensor_tensor(tile_of(hT, t), bank(PRE), pos2[:].rearrange("p b t -> p (b t)"),
                                        ALU.add).then_inc(h_done, 1)

            def centre(t):
                dve.wait_ge(mean_done, t + 1)
                nc.vector.tensor_tensor(cen[:], tile_of(hT, t), bank(PRE), ALU.subtract).then_inc(cen_done, 1)

            def normal(t, par):
                dve.wait_ge(rstd_done, t + 1)
                nc.vector.tensor_tensor(Y[par][0][:], cen[:], rstd[:], ALU.mult).then_inc(y0_done, 1)

            def step(x):
                dve.wait_ge(soft_done, 3 * x + 3)
                if not (isinstance(x, int) and x == 0):
                    dve.wait_ge(dtlo_done, x)
                nc.vector.scalar_tensor_tensor(out=dt[:], in0=zpre[:], scalar=0.0, in1=zexp[:], op0=ALU.max,
                                               op1=ALU.add).then_inc(dt_done, 1)

            def low_dx(x):
                dve.wait_ge(hi_done, 2 * x + 2)
                if not (isinstance(x, int) and x == 0):
                    dve.wait_ge(s_in, 128 * x)
                nc.vector.tensor_tensor(dx_lo[:], dx[:], dx_hi[:].bitcast(f32), ALU.subtract).then_inc(dxlo_done, 1)

            def add_skip(x, par, layer):
                dve.wait_ge(nsum_done, 4 * x + 4)
                if layer == 1:
                    dve.wait_ge(linb_done, x - 1)
                nc.vector.scalar_tensor_tensor(out=skip[:], in0=Y[par][layer][:], scalar=dsk(layer), in1=bank(NSUM),
                                               op0=ALU.mult, op1=ALU.add).then_inc(skip_done, 1)

            def residual(t):
                dve.wait_ge(dec_done, t + 1)
                nc.vector.scalar_tensor_tensor(out=tile_of(hT, t), in0=bank(POST), scalar=bdec, in1=tile_of(hT, t),
                                               op0=ALU.add, op1=ALU.add).then_inc(resid_done, 1)

            embed(0)
            centre(0)
            normal(0, 0)
            step(0)
            low_dx(0)

            def slot(q, c):
                s, par = 4 * q + c, c % 2
                nxt, prv = (c + 1) % 4, (c + 3) % 4
                middle = c in (1, 2)

                def drive(i):
                    dve.wait_ge(rep_dx, 16 * s + i + 1)
                    nc.vector.tensor_tensor(bank(DX + i % 3), bank(DX + i % 3), B[par][:], ALU.mult).then_inc(b_done, 1)

                dve.wait_ge(b_ready, s + 1)
                drive(0)
                for i in range(GROUPS):
                    if i + 1 < GROUPS:
                        drive(i + 1)
                    dve.wait_ge(exp_done, 16 * s + i + 1)
                    dve.wait_ge(b_done, 16 * s + i + 1)
                    if not (starts(q) and c == 0 and i < 4):
                        dve.wait_ge(hc_done, 16 * s + i - 3)
                    nc.vector.tensor_tensor_scan(state[i % 4][:], decay[i % 4][:].rearrange("p b t -> p (b t)"),
                                                 bank(DX + i % 3), 0.0, ALU.mult, ALU.add).then_inc(scan_done, 1)
                    if not (starts(q) and c == 0):
                        if i == 3:
                            add_skip(s - 1, prv % 2, prv // 2)
                        if i == 10 and not middle:
                            residual(posted_tile(q, c))
                    if last(q, c):
                        continue
                    if not middle:
                        if i == 1:
                            embed(prepared_tile(q, c))
                        if i == 2:
                            centre(prepared_tile(q, c))
                        if i == 6:
                            normal(prepared_tile(q, c), nxt % 2)
                    if i == 10:
                        step(s + 1)
                    if i == 13:
                        low_dx(s + 1)

            run_slots(dve, slot)
            add_skip(15, 1, 1)
            residual(TILES - 1)

            wide = [CHUNK, 4, EXPERTS, EXPERTS]
            with dve.Fori(0, TILES) as t:
                dve.wait_ge(m_mean, t + 1)
                nc.vector.tensor_tensor(cen[:], tile_of(hT, t), bank(7), ALU.subtract).then_inc(m_cen, 1)
                nc.vector.tensor_copy(cen_h[:], tile_of(hT, t)).then_inc(m_h, 1)
                dve.wait_ge(m_rstd, t + 1)
                nc.vector.tensor_tensor(xn[:], cen[:], rstd[:], ALU.mult).then_inc(m_xn, 1)
                dve.wait_ge(logit_done, t + 1)
                lg = bank(7, 4 * EXPERTS, CHUNK).rearrange("p (k e) -> p k e", k=4)
                steps = [0]
                STEPS = 9

                def link(ins):
                    steps[0] += 1
                    ins.then_inc(gate_step, 1)
                    dve.wait_ge(gate_step, t * STEPS + steps[0])

                link(nc.vector.tensor_tensor(prob[:], lg, brr[0:CHUNK, :].unsqueeze(1).to_broadcast([CHUNK, 4, EXPERTS]), ALU.add))
                link(nc.vector.tensor_reduce(lmax[:], prob[:], AX.X, ALU.max))
                nc.vector.tensor_tensor(prob[:], prob[:], lmax[:].unsqueeze(2).to_broadcast([CHUNK, 4, EXPERTS]),
                                        ALU.subtract).then_inc(shift_done, 1)
                dve.wait_ge(pexp_done, t + 1)
                link(nc.vector.tensor_reduce(lsum[:], prob[:], AX.X, ALU.add))
                link(nc.vector.reciprocal(lrec[:], lsum[:]))
                link(nc.vector.tensor_tensor(prob[:], prob[:], lrec[:].unsqueeze(2).to_broadcast([CHUNK, 4, EXPERTS]), ALU.mult))
                other, own = prob[:].unsqueeze(2).to_broadcast(wide), prob[:].unsqueeze(3).to_broadcast(wide)
                nc.vector.tensor_tensor(gt[:], other, own, ALU.is_gt)
                link(nc.vector.tensor_tensor(eq[:], other, own, ALU.is_equal))
                for k in range(4):
                    ins = nc.vector.tensor_tensor(eq[:, k, :, :], eq[:, k, :, :], earl[0:CHUNK, :, :], ALU.mult)
                link(ins)
                link(nc.vector.tensor_tensor(gt[:], gt[:], eq[:], ALU.add))
                link(nc.vector.tensor_reduce(rank[:], gt[:], AX.X, ALU.add))
                nc.vector.scalar_tensor_tensor(out=gate[:], in0=rank[:], scalar=TOP - 0.5, in1=prob[:], op0=ALU.is_lt,
                                               op1=ALU.mult).then_inc(gate_done, 1)
                assert steps[0] == STEPS
                dve.wait_ge(init_ready, t + 1)
                dve.wait_ge(gate_done, t + 1)
                for e in range(EXPERTS):
                    dve.wait_ge(down_done, t * EXPERTS + e + 1)
                    if e:
                        dve.wait_ge(comb_done, t * EXPERTS + e)
                    for k in range(4):
                        ins = nc.vector.scalar_tensor_tensor(
                            out=acc[:, k, :], in0=psum[0:CHUNK, (4 + e % 2) * BANK + 128 * k:(4 + e % 2) * BANK + 128 * k + 128],
                            scalar=gate[:, k, e:e + 1], in1=acc[:, k, :], op0=ALU.mult, op1=ALU.add)
                    ins.then_inc(comb_done, 1)

        @block.tensor
        def _(pe):
            pe.wait_ge(param_in, 16 * PARAM_DMAS)
            pe.wait_ge(consts, 1 + 4 + 1 + 2 * LAYERS)
            pe.wait_ge(tok_in, 32)

            def tokens(t, prepared):
                if prepared is not None:
                    pe.wait_ge(c_ready, prepared)
                nc.tensor.matmul(bank(PRE), wtok[:], rows[:].rearrange("p b t -> p (b t)")[:, bass.ds(t * TOK, TOK)],
                                 start=True, stop=True).then_inc(tok_done, 1)

            def mean(t):
                pe.wait_ge(h_done, t + 1)
                nc.tensor.matmul(bank(PRE), mean_w[:], tile_of(hT, t), start=True, stop=True).then_inc(mean_done, 1)

            def variance(t):
                pe.wait_ge(sq_done, t + 1)
                nc.tensor.matmul(bank(PRE), mean_w[:], sq[:], start=True, stop=True).then_inc(var_done, 1)

            def project_dt(x, t, par, layer):
                if layer == 0:
                    pe.wait_ge(y0_done, t + 1)
                else:
                    pe.wait_ge(linb_done, x - 1)
                    pe.wait_ge(c_ready, x)
                nc.tensor.matmul(bank(PRE), wdt[:, layer, :], Y[par][layer][:], start=True, stop=True).then_inc(wdt_done, 1)

            def project_b(x, par, layer):
                pe.wait_ge(z_done, x + 1)
                nc.tensor.matmul(bank(PRE), wb[:, layer, :, :].rearrange("p n j -> p (n j)"), Y[par][layer][:],
                                 start=True, stop=True).then_inc(wb_done, 1)

            def project_c(x, par, layer):
                pe.wait_ge(b_ready, x + 1)
                nc.tensor.matmul(bank(PRE), wc[:, layer, :, :].rearrange("p n j -> p (n j)"), Y[par][layer][:],
                                 start=True, stop=True).then_inc(wc_done, 1)

            def linear(x, layer):
                pe.wait_ge(relu_done, x + 1)
                nc.tensor.matmul(bank(POST), wlin[:, layer, :], act_y[:], start=True, stop=True).then_inc(lin_done, 1)

            def decode(x):
                pe.wait_ge(linb_done, x + 1)
                nc.tensor.matmul(bank(POST), wdec[:], lin1[:], start=True, stop=True).then_inc(dec_done, 1)

            def sum_states(s, k):
                pe.wait_ge(hc_done, 16 * s + 4 * k + 4)
                if k == 0 and not (isinstance(s, int) and s == 0):
                    pe.wait_ge(skip_done, s)
                for i in range(4 * k, 4 * k + 4):
                    quad = group(i) // 4
                    ins = nc.tensor.matmul(psum[32 * quad:32 * quad + 32, NSUM * BANK:NSUM * BANK + TOK],
                                           gath[:, group(i) % 4, :], hc[i % 8][:], start=(k == 0), stop=(k == 3))
                ins.then_inc(nsum_done, 1)

            tokens(0, None)
            mean(0)
            variance(0)
            project_dt(0, 0, 0, 0)
            project_b(0, 0, 0)
            project_c(0, 0, 0)

            def slot(q, c):
                s, par = 4 * q + c, c % 2
                nxt, prv = (c + 1) % 4, (c + 3) % 4
                middle = c in (1, 2)
                first = starts(q) and c == 0
                pe.wait_ge(s_in, 128 * (s + 1))
                for i in range(GROUPS):
                    g = group(i)
                    if not (first and i < 2):
                        pe.wait_ge(exp_done, 16 * s + i - 1)
                    nc.tensor.matmul(bank(DT + i % 2), spreadr[:, g % 8, :], S_dt[par][:, g // 8, :], start=True,
                                     stop=True).then_inc(rep_dt, 1)
                    if not (first and i < 3):
                        pe.wait_ge(scan_done, 16 * s + (i - 2 if i >= 3 else (0, -2, -1)[i]))
                    nc.tensor.matmul(bank(DX + i % 3), spreadr[:, g % 8, :], S_dx[par][:, g // 8, :], start=True,
                                     stop=True).then_inc(rep_dx, 1)
                    if not first:
                        if i == 3:
                            sum_states(s - 1, 3)
                        if i == 6:
                            linear(s - 1, prv // 2)
                        if i == 9 and not middle:
                            decode(s - 1)
                    if i in (7, 11, 15):
                        sum_states(s, i // 4 - 1)
                    if last(q, c):
                        continue
                    if not middle:
                        t = prepared_tile(q, c)
                        if i == 1:
                            tokens(t, s + 1)
                        if i == 2:
                            mean(t)
                        if i == 5:
                            variance(t)
                    if i == 8:
                        project_dt(s + 1, prepared_tile(q, c), nxt % 2, nxt // 2)
                    if i == 9:
                        project_b(s + 1, nxt % 2, nxt // 2)
                    if i == 10:
                        project_c(s + 1, nxt % 2, nxt // 2)

            run_slots(pe, slot)
            sum_states(15, 3)
            linear(15, 1)
            decode(15)

            pe.wait_ge(resid_done, TILES)
            pe.wait_ge(moe_in, 48)
            with pe.Fori(0, TILES) as t:
                def up(e):
                    for f in range(FCH):
                        if e:
                            pe.wait_ge(hid_done, t * 32 + 4 * e + f - 3)
                        nc.tensor.matmul(bank(f), w1[:, e, 128 * f:128 * f + 128], xn[:], start=True,
                                         stop=True).then_inc(up_done, 1)

                def down(e):
                    pe.wait_ge(hid_done, t * 32 + 4 * e + 4)
                    if e >= 2:
                        pe.wait_ge(comb_done, t * EXPERTS + e - 1)
                    for k in range(4):
                        for f in range(FCH):
                            ins = nc.tensor.matmul(
                                psum[0:CHUNK, (4 + e % 2) * BANK + 128 * k:(4 + e % 2) * BANK + 128 * k + 128],
                                hid[e % 2][f][:, CHUNK_AT[k]:CHUNK_AT[k] + CHUNK], w2[:, e, f, :],
                                start=(f == 0), stop=(f == FCH - 1))
                    ins.then_inc(down_done, 1)

                nc.tensor.matmul(bank(7), mean_w[:], tile_of(hT, t), start=True, stop=True).then_inc(m_mean, 1)
                pe.wait_ge(m_sq, t + 1)
                nc.tensor.matmul(bank(7), mean_w[:], sq[:], start=True, stop=True).then_inc(m_var, 1)
                pe.wait_ge(m_xn, t + 1)
                for k in range(4):
                    ins = nc.tensor.matmul(psum[0:CHUNK, 7 * BANK + 8 * k:7 * BANK + 8 * k + 8],
                                           xn[:, CHUNK_AT[k]:CHUNK_AT[k] + CHUNK], wr[:], start=True, stop=True)
                ins.then_inc(logit_done, 1)
                up(0)
                pe.wait_ge(gate_done, t + 1)
                for k in range(4):
                    ins = nc.tensor.transpose(psum[0:EXPERTS, 7 * BANK + CHUNK * k:7 * BANK + CHUNK * (k + 1)],
                                              gate[:, k, :], ident[0:CHUNK, 0:CHUNK])
                ins.then_inc(gateT_done, 1)
                pe.wait_ge(gateT_ready, t + 1)
                pe.wait_ge(m_h, t + 1)
                for k in range(4):
                    dst = psum[0:CHUNK, 6 * BANK + 128 * k:6 * BANK + 128 * k + 128]
                    nc.tensor.matmul(dst, cen_h[:, CHUNK_AT[k]:CHUNK_AT[k] + CHUNK], ident[:], start=True, stop=False)
                    ins = nc.tensor.matmul(dst, gateT[:, k, :], b2[:], start=False, stop=True)
                ins.then_inc(init_done, 1)
                for e in range(1, EXPERTS):
                    up(e)
                    down(e - 1)
                down(EXPERTS - 1)
                pe.wait_ge(hid_done, (t + 1) * 32)
                pe.wait_ge(comb_done, (t + 1) * EXPERTS)


def kernel(**inputs):
    import concourse.bacc as bacc
    from concourse.bass_utils import run_bass_kernel_spmd

    g = {k: np.asarray(v) for k, v in inputs.items()}
    c = np.ascontiguousarray
    at = lambda n: g["L0_attn_" + n]
    fn = lambda n: g["L0_ffn_" + n]
    samples = (LENGTH + 1) * STRIDE
    cols = [at("bdt").T, np.repeat(at("bB"), GCH, axis=1).T, np.repeat(at("bC"), GCH, axis=1).T, at("D_skip").T, at("blin").T,
            at("bdec")[:, None], np.full((128, 1), EPS, np.float32), np.zeros((128, 1), np.float32), np.ones((128, 1), np.float32)]
    p = np.arange(128)
    spread = np.zeros((128, 8, 128), np.float32)
    gather = np.zeros((128, 4, 32), np.float32)
    for r in range(8):
        spread[:, r, :] = (p[:, None] % 64) == 8 * r + p[None, :] % 8
    for r in range(4):
        gather[:, r, :] = p[None, :32] == 8 * r + p[:, None] % 8
    earlier = np.broadcast_to(np.tri(EXPERTS, k=-1, dtype=np.float32), (128, EXPERTS, EXPERTS))
    arrays = {
        "x_rows": g["x"][:, :samples, 0].reshape(SEQS, LENGTH + 1, STRIDE).transpose(2, 0, 1),
        "w_tok": g["L0_tok_W"].T,
        "pos": g["L0_tok_pos_embed"][0, :LENGTH].T,
        "a_cols": at("A").reshape(LAYERS, GROUPS, GCH, STATES).transpose(3, 2, 0, 1).reshape(128, LAYERS, GROUPS),
        "w_dt": at("Wdt").transpose(1, 0, 2), "w_b": at("WB").transpose(1, 0, 2), "w_c": at("WC").transpose(1, 0, 2),
        "w_lin": at("Wlin").transpose(1, 0, 2), "w_dec": at("Wdec"),
        "vecs": np.concatenate(cols, axis=1),
        "w_r": fn("Wr"), "b_r": np.broadcast_to(fn("br"), (128, EXPERTS)),
        "w_1": fn("W1").transpose(1, 0, 2), "b_1": fn("b1").reshape(EXPERTS, FCH, 128).transpose(2, 0, 1),
        "w_2": fn("W2").reshape(EXPERTS, FCH, 128, 128).transpose(2, 0, 1, 3), "b_2": fn("b2"),
        "spread": spread, "gather": gather, "eye": np.eye(128, dtype=np.float32), "earlier": earlier,
    }
    arrays = {k: c(v) for k, v in arrays.items()}
    nc = bacc.Bacc("TRN2", target_bir_lowering=False, num_devices=1)
    args = [nc.dram_tensor(k, v.shape, mybir.dt.from_np(v.dtype), kind="ExternalInput").ap() for k, v in arrays.items()]
    out = nc.dram_tensor("out", (TOKENS, CHANNELS), mybir.dt.float32, kind="ExternalOutput").ap()
    audio_tower(nc, *args, out)
    r = run_bass_kernel_spmd(nc, [arrays], core_ids=[0])
    return r.results[0]["out"].reshape(SEQS, LENGTH, CHANNELS)
```

```python
import numpy as np
import concourse.bass as bass
from concourse import mybir
from contextlib import ExitStack

SEQS, LENGTH, CHANNELS, STATES, LAYERS = 16, 249, 128, 16, 2
PATCH, STRIDE = 64, 32
EXPERTS, HIDDEN, TOP = 8, 512, 2
PER_TILE = 2
TOK = PER_TILE * LENGTH
TILES = SEQS // PER_TILE
TOKENS = SEQS * LENGTH
SLOTS = TILES * LAYERS
GROUPS = CHANNELS // (128 // STATES)
GCH = CHANNELS // GROUPS
BANK = 512
CHUNK = 125
CHUNKS = 4
CHUNK_TOK = [125, 125, 125, TOK - 3 * CHUNK]
FCH = HIDDEN // 128
EPS = 1e-5
CAP = -(-TOKENS // 128) * 128 + 128
BLOCKS = (TOKENS * TOP) // 128 + EXPERTS
SPARE = EXPERTS * CAP
FEWEST = -(-TOKENS * TOP // 128)
QUEUE_ROWS = SPARE + (BLOCKS - FEWEST) * 128
ROW = CHANNELS + 1
RESULT = TILES * CHUNKS * CHUNK
NOWHERE = 1 << 20
UP, DOWN = HIDDEN + FCH, HIDDEN + CHANNELS


def audio_tower(nc, x_rows, w_tok, pos, a_cols, w_dt, w_b, w_c, w_lin, w_dec, vecs, w_r, b_r, w_up, w_down,
                spread, gather, eye, before, small, places, out):
    f32, f32r, bf16, i32 = mybir.dt.float32, mybir.dt.float32r, mybir.dt.bfloat16, mybir.dt.int32
    queue = nc.dram_tensor("queue", (QUEUE_ROWS, ROW), f32, kind="Internal").ap()
    results = nc.dram_tensor("results", (TOP * RESULT, CHANNELS), f32, kind="Internal").ap()
    ALU, ACT, AX = mybir.AluOpType, mybir.ActivationFunctionType, mybir.AxisListType

    with ExitStack() as ctx:
        def sb(name, shape, dt=f32):
            return ctx.enter_context(nc.sbuf_tensor(name, shape, dt))

        def sem(name):
            return ctx.enter_context(nc.semaphore(name))

        rows = sb("rows", [PATCH, SEQS, LENGTH])
        wtok = sb("wtok", [PATCH, CHANNELS])
        pos2 = sb("pos2", [128, PER_TILE, LENGTH])
        acol = sb("acol", [128, LAYERS, GROUPS])
        wdt = sb("wdt", [128, LAYERS, 128])
        wb16 = sb("wb16", [128, LAYERS, STATES])
        wc16 = sb("wc16", [128, LAYERS, STATES])
        wb = sb("wb", [128, LAYERS, STATES, GCH])
        wc = sb("wc", [128, LAYERS, STATES, GCH])
        wlin = sb("wlin", [128, LAYERS, 128])
        wdec = sb("wdec", [128, 128])
        NV = 14
        vec = sb("vec", [128, NV])
        bdt, bbr, bcr, dsk, bln = (lambda l, k=k: vec[:, 2 * k + l:2 * k + l + 1] for k in range(5))
        bdec, epsc, zero, one = (vec[:, 10 + k:11 + k] for k in range(4))
        spread_in = sb("spread_in", [128, 8, 128])
        spreadr = sb("spreadr", [128, 8, 128], f32r)
        gath = sb("gath", [128, 4, 32])
        mean_w = sb("mean_w", [128, 128])
        ident = sb("ident", [128, 128])
        wr = sb("wr", [128, EXPERTS])
        brr = sb("brr", [128, EXPERTS])
        moe_all = sb("moe_all", [128, EXPERTS * (UP + DOWN)])
        up_all = moe_all[:, 0:EXPERTS * UP].rearrange("p (e n) -> p e n", e=EXPERTS)
        down_all = moe_all[:, EXPERTS * UP:].rearrange("p (e n) -> p e n", e=EXPERTS)
        before_in = sb("before_in", [CHUNK, CHUNK])
        beforeb = sb("beforeb", [CHUNK, CHUNK], bf16)
        onesb = sb("onesb", [CHUNK, 128], bf16)
        sml = sb("sml", [128, 6 * EXPERTS])
        first_of = sml[:, 0:8]
        region = sml[:, 8:16]
        valid = sml[0:CHUNK, 16:20]
        number = sml[:, 20:21]
        spare = sml[:, 21:22]
        expert = sml[:, 24:32]
        plc = sb("plc", [CHUNK, TOP, CHUNKS])

        hT = sb("hT", [128, TILES * TOK])
        Y = [sb(f"Y{l}", [128, TOK]) for l in range(LAYERS)]
        B = [sb(f"B{p}", [128, TOK]) for p in range(2)]
        C = [sb(f"C{p}", [128, TOK]) for p in range(2)]
        S_dt = [sb(f"S_dt{p}", [128, 2, TOK], f32r) for p in range(2)]
        S_dx = [sb(f"S_dx{p}", [128, 2, TOK], f32r) for p in range(2)]
        decay = [sb(f"decay{k}", [128, PER_TILE, LENGTH]) for k in range(4)]
        state = [sb(f"state{k}", [128, TOK]) for k in range(4)]
        hc_all = sb("hc_all", [128, 8 * TOK])
        hc = [hc_all[:, k * TOK:(k + 1) * TOK] for k in range(8)]
        cen_w = sb("cen_w", [128, 128])
        dskip = sb("dskip", [128, LAYERS, 128])
        act_y = sb("act_y", [128, TOK])
        lin1 = sb("lin1", [128, TOK])
        zpre = sb("zpre", [128, TOK])
        zexp = sb("zexp", [128, TOK])
        dt = sb("dt", [128, TOK])
        dx = sb("dx", [128, TOK])
        dt_hi, dt_lo, dx_hi, dx_lo = (sb(n, [128, TOK], f32r) for n in ("dt_hi", "dt_lo", "dx_hi", "dx_lo"))
        cen = sb("cen", [128, TOK])
        sq = sb("sq", [128, TOK])
        rstd = sb("rstd", [128, TOK])
        h_s = sb("h_s", [128, CHUNKS * CHUNK])
        rcen = sb("rcen", [128, TOK])
        rsq = sb("rsq", [128, TOK])
        rrstd = sb("rrstd", [128, TOK])
        xn = sb("xn", [128, CHUNKS * CHUNK])
        E3 = [CHUNK, CHUNKS, EXPERTS]
        prob = sb("prob", E3)
        small_k = sb("small_k", [CHUNK, CHUNKS])
        top = sb("top", [CHUNK, TOP, CHUNKS])
        key = sb("key", [CHUNK, CHUNKS])
        same = sb("same", E3)
        hot = [sb(f"hot{j}", E3) for j in range(TOP)]
        left = sb("left", E3)
        taken = sb("taken", E3, bf16)
        fill = sb("fill", [128, EXPERTS])
        seat = sb("seat", E3)
        pick = sb("pick", E3)
        seat_f = sb("seat_f", [CHUNK, TOP, CHUNKS])
        seats = sb("seats", [CHUNK, TOP, CHUNKS], i32)
        staged = sb("staged", [CHUNK, TOP, CHUNKS, ROW])
        gates = sb("gates", [CHUNK, TILES, TOP, CHUNKS])
        htok = sb("htok", [CHUNK, TILES, CHUNKS * CHANNELS])
        padding = sb("padding", [128, ROW])
        ends = sb("ends", [128, EXPERTS], i32)
        tab8 = [sb(f"tab8{k}", [128, EXPERTS]) for k in range(5)]
        blocks_i = sb("blocks_i", [128, EXPERTS], i32)
        tab = sb("tab", [128, 3])
        table = sb("table", [1, 2, BLOCKS], i32)
        xg = [sb(f"xg{b}", [128, ROW]) for b in range(4)]
        goes = sb("goes", [128, BLOCKS], i32)
        held = sb("held", [1, 1])
        goes_now = [sb(f"goes_now{b}", [128, 1], i32) for b in range(2)]

        def lay(store, at, n, parts=128):
            return [store[0:parts, at + b * n:at + (b + 1) * n] for b in range(2)]

        xT = lay(hT, 0, 128)
        ysb = lay(hT, 256, CHANNELS)
        up_w = lay(hc_all, 0, UP)
        down_w = lay(hc_all, 2 * UP, DOWN)
        hid = [v.rearrange("p (f m) -> p f m", f=FCH) for v in lay(hc_all, 2 * (UP + DOWN), FCH * 128)]
        yb = moe_all[0:CHUNK, 0:TILES * TOP * CHUNKS * CHANNELS].rearrange("p (t j k d) -> p t j k d", t=TILES, j=TOP, k=CHUNKS)

        psum = ctx.enter_context(nc.psum_tensor("psum", [128, 8 * BANK], f32))

        def bank(k, n=TOK, p=128):
            return psum[0:p, k * BANK:k * BANK + n]

        def up_out(b, f):
            at = (2 * b + f // 2) * BANK + 128 * (f % 2)
            return psum[:, at:at + 128]

        DT, DX, NSUM, POST, PRE = 0, 2, 5, 6, 7

        param_in, tok_in, moe_in = sem("param_in"), sem("tok_in"), sem("moe_in")
        consts = sem("consts")
        rep_dt, rep_dx = sem("rep_dt"), sem("rep_dx")
        exp_done, b_done, scan_done = sem("exp_done"), sem("b_done"), sem("scan_done")
        hc_done, nsum_done = sem("hc_done"), sem("nsum_done")
        diag_done, abs_done, zexp_done, zlog_done = (sem(n) for n in ("diag_done", "abs_done", "zexp_done", "zlog_done"))
        relu_done, lin_done, linb_done = sem("relu_done"), sem("lin_done"), sem("linb_done")
        dec_done, resid_done = sem("dec_done"), sem("resid_done")
        tok_done, h_done, cenm_done, cen_done = sem("tok_done"), sem("h_done"), sem("cenm_done"), sem("cen_done")
        sq_done, var_done, ln_done, rstd_done, y0_done = (sem(n) for n in ("sq_done", "var_done", "ln_done", "rstd_done", "y0_done"))
        wdt_done, z_done, dt_done, dx_done = (sem(n) for n in ("wdt_done", "z_done", "dt_done", "dx_done"))
        hi_done, dtlo_done, dxlo_done, s_in = sem("hi_done"), sem("dtlo_done"), sem("dxlo_done"), sem("s_in")
        wb_done, b_ready, wc_done, c_ready = (sem(n) for n in ("wb_done", "b_ready", "wc_done", "c_ready"))

        (r_cenm, r_cen, r_sq, r_var, r_ln, r_rstd, r_xn, r_logit, r_shift, r_pexp, r_step, r_mask, r_prefix, r_seats,
         r_trh, r_htok, r_trx, r_staged, r_places) = (sem("r_" + n) for n in (
             "cenm", "cen", "sq", "var", "ln", "rstd", "xn", "logit", "shift", "pexp", "step", "mask", "prefix", "seats",
             "trh", "htok", "trx", "staged", "places"))
        r_pick, r_sum, r_moved = (sem("r_" + n) for n in ("pick", "sum", "moved"))
        scattered, spare_in, pad_set, padded = (sem(n) for n in ("scattered", "spare_in", "pad_set", "padded"))
        t_step, t_cols, t_rows, t_ready = (sem(n) for n in ("t_step", "t_cols", "t_rows", "t_ready"))
        xg_in = [sem(f"xg_in{b}") for b in range(4)]
        goes_set = sem("goes_set")
        turned, xT_ready, goes_ready, up_copied, down_copied = (sem(n) for n in ("turned", "xT_ready", "goes_ready", "up_copied", "down_copied"))
        up_done, relu_a, relu_v, down_done, y_ready = (sem(n) for n in ("up_done", "relu_a", "relu_v", "down_done", "y_ready"))
        stored = [sem(f"stored{b}") for b in range(2)]
        yb_in = [sem(f"yb_in{b}") for b in range(4)]
        half_sum, summed = sem("half_sum"), sem("summed")
        out_done = sem("out_done")

        block = ctx.enter_context(nc.Block())

        def run_slots(engine, slot):
            def pair(t, a, b, c):
                slot(2 * t - 1, layer=0, after=(t - 2, 1), project=(2 * t, 1, 2 * t - 2), late=False, embed=t + 1 if a else None,
                     route=(t - 2, None, t - 3 if b else None))
                if c:
                    slot(2 * t, layer=1, after=(t, 0), project=(2 * t + 1, 0, t + 2), late=False, embed=None,
                         route=(None, t - 2, t - 3 if b else None))

            slot(0, layer=0, after=None, project=(1, 0, 2), late=True, embed=1)
            slot(1, layer=0, after=(0, 0), project=(2, 1, 1), late=True, embed=2)
            slot(2, layer=1, after=(1, 0), project=(3, 0, 3), late=False, embed=None)
            pair(2, True, False, True)
            with engine.Fori(3, TILES - 1) as t:
                pair(t, True, True, True)
            pair(TILES - 1, False, True, False)
            h = 2 * TILES - 2
            slot(h, layer=1, after=(TILES - 1, 0), project=(h + 1, 1, h), late=True, embed=None,
                 route=(None, TILES - 3, TILES - 4))
            slot(h + 1, layer=1, after=(TILES - 2, 1), project=None, late=False, embed=None,
                 route=(TILES - 2, None, TILES - 3))

        def parity_of(h, layer):
            return h % 2 if isinstance(h, int) else 1 - layer

        def group(i):
            return (i % 4) * 4 + i // 4

        def scatter_half(h, layer):
            return 1 - parity_of(h, layer)

        def tile_of(tensor, t):
            return tensor[:, bass.ds(t * TOK, TOK)]

        def early(x, n):
            return isinstance(x, int) and x < n

        def place(late):
            at = dict(wdt=0, z=1, abs=2, wb=3, exp=3, b=4, ln=4, dt=5, wc=5, c=6, dt_hi=6, dx=6, dt_lo=7, dx_hi=8, dx_lo=9,
                      sum3=2, relu=4, diag=6, lin=8, lin_b=9, dec=10, resid=12,
                      tok=9, h=10, cenm=12, cen=13, sq=13, var=14, lnv=14, rstd=15, normal=15)
            at.update(r_cenm=13, r_cen=14, r_sq=15,
                      r_var=1, r_ln=2, r_rstd=3, r_xn=4, r_logit=6, r_shift=6, r_pexp=7, r_prob=8, r_top1=9, r_top2=10,
                      scatters=(0, 3, 6, 9), r_mask=11, r_trh=9, r_htok=10, r_trx=10, r_staged=12, r_prefix=12, r_seats=14)
            if late:
                at.update(wdt=10, z=11, wb=11, abs=12, b=12, wc=12, exp=13, ln=14, c=14, dt=15, dx=15, dt_hi=15, dt_lo=15,
                          dx_hi=15, dx_lo=15, r_trh=3, r_htok=4, r_trx=5, r_staged=9, scatters=(0, 2, 4, 6),
                          tok=0, h=1, cenm=2, cen=3, sq=4, var=5, lnv=6, rstd=7, normal=8)
            return at

        PARAM_DMAS = 19
        CONSTS = 2 + 4 + 1 + 2 * LAYERS + LAYERS + 5

        @block.sync
        def _(sp):
            for dst, src in ((wtok[:], w_tok), (wdt[:], w_dt), (wb16[:], w_b), (wc16[:], w_c), (vec[:], vecs),
                             (acol[:], a_cols), (pos2[:, 0, :], pos), (pos2[:, 1, :], pos), (spread_in[:], spread),
                             (gath[:], gather), (wlin[:], w_lin), (wdec[:], w_dec), (ident[:], eye), (before_in[:], before),
                             (wr[:], w_r), (brr[:], b_r), (sml[:], small), (plc[:, 0, :], places[:, 0, :]), (plc[:, 1, :], places[:, 1, :])):
                sp.dma_start(dst, src).then_inc(param_in, 16)
            sp.dma_start(up_all[:], w_up).then_inc(moe_in, 16)
            sp.dma_start(down_all[:], w_down).then_inc(moe_in, 16)
            sp.wait_ge(pad_set, 2)
            for k in range(BLOCKS - FEWEST):
                sp.dma_start(queue[SPARE + 128 * k:SPARE + 128 * k + 128, :], padding[:]).then_inc(spare_in, 16)

            for k in range(TOK, CHUNKS * CHUNK):
                none = results.rearrange("(a r) d -> a r d", r=CHUNKS * CHUNK)[:, k, :]
                sp.dma_start(none, padding[0:TOP * TILES, 0:CHANNELS]).then_inc(spare_in, 16)

            def place_split(x, par):
                first_hi, second_hi, lo_x = ((2 * x + 1, 2 * x + 2, x + 1) if isinstance(x, int) else
                                             (sp.snap(2 * x + 1), sp.snap(2 * x + 2), sp.snap(x + 1)))
                for n, (S, hi, lo, lo_done) in enumerate(((S_dt, dt_hi, dt_lo, dtlo_done), (S_dx, dx_hi, dx_lo, dxlo_done))):
                    sp.wait_ge(hi_done, (first_hi, second_hi)[n])
                    sp.dma_start(S[par][0:64, 0, :].bitcast(f32), hi[0:64, :].bitcast(f32)).then_inc(s_in, 16)
                    sp.dma_start(S[par][64:128, 1, :].bitcast(f32), hi[64:128, :].bitcast(f32)).then_inc(s_in, 16)
                    sp.wait_ge(lo_done, lo_x)
                    sp.dma_start(S[par][64:128, 0, :].bitcast(f32), lo[0:64, :].bitcast(f32)).then_inc(s_in, 16)
                    sp.dma_start(S[par][0:64, 1, :].bitcast(f32), lo[64:128, :].bitcast(f32)).then_inc(s_in, 16)

            place_split(0, 0)

            def slot(h, layer, after, project, late, embed, route=(None, None, None)):
                if project:
                    place_split(project[0], 1 - parity_of(h, layer))

            run_slots(sp, slot)

            sp.wait_ge(pad_set, 3)
            for e in range(EXPERTS):
                end = sp.value_load(ends[0:1, e:e + 1], min_val=0, max_val=SPARE - 128)
                sp.dma_start(queue[bass.ds(end, 128), :], padding[:]).then_inc(padded, 16)
            sp.wait_ge(scattered, 16 * TILES * CHUNKS * TOP)
            sp.wait_ge(padded, 16 * EXPERTS)
            sp.wait_ge(spare_in, 16 * (BLOCKS - FEWEST + CHUNKS * CHUNK - TOK))
            sp.wait_ge(t_ready, 1)

            def load(m, b, free):
                if isinstance(m, int):
                    row = sp.value_load(table[0:1, 0, m:m + 1], min_val=0, max_val=QUEUE_ROWS - 128)
                else:
                    row = sp.value_load(table[0:1, 0, bass.ds(m, 1)], min_val=0, max_val=QUEUE_ROWS - 128)
                if free is not None:
                    sp.wait_ge(turned, free)
                    sp.wait_ge(goes_ready, free)
                sp.dma_start(xg[b][:], queue[bass.ds(row, 128), :]).then_inc(xg_in[b], 16)

            for m in range(4):
                load(m, m, None)
            with sp.Fori(1, BLOCKS // 4) as j:
                free = [sp.snap(4 * j - 3 + b) for b in range(4)]
                for b in range(4):
                    load(4 * j + b, b, free[b])
            for m in range(BLOCKS - 2, BLOCKS):
                load(m, m % 4, m - 3)

            for b in range(2):
                sp.wait_ge(stored[b], 16 * (BLOCKS // 2))
            for t in range(TILES):
                if t >= 4:
                    sp.wait_ge(summed, t - 3)
                tile = results.rearrange("(j t r) d -> t j r d", j=TOP, t=TILES)
                for j in range(TOP):
                    src = tile[t, j, :, :].rearrange("(k p) d -> p k d", k=CHUNKS)
                    sp.dma_start(yb[:, t, j, :, :], src).then_inc(yb_in[t % 4], 16)

        @block.gpsimd
        def _(pool):
            pool.dma_start(rows[0:STRIDE, :, :], x_rows[:, :, 0:LENGTH]).then_inc(tok_in, 16)
            pool.dma_start(rows[STRIDE:PATCH, :, :], x_rows[:, :, 1:LENGTH + 1]).then_inc(tok_in, 16)

            def low_dt(x):
                pool.wait_ge(hi_done, 2 * x + 1)
                if not early(x, 1):
                    pool.wait_ge(s_in, 128 * x)
                nc.gpsimd.tensor_tensor(dt_lo[:], dt[:], dt_hi[:].bitcast(f32), ALU.subtract).then_inc(dtlo_done, 1)

            low_dt(0)

            def scatter(t, j, k):
                if j == 0 and k == 0:
                    pool.wait_ge(r_seats, t + 1)
                    pool.wait_ge(r_staged, 2 * t + 2)
                    pool.wait_ge(r_places, t + 1)
                    if not isinstance(t, int):
                        nc.gpsimd.tensor_tensor(held[:], ident[0:1, 0:1], ident[0:1, 0:1], ALU.mult)
                n = CHUNK_TOK[k]
                nc.gpsimd.indirect_dma_start(out=queue, out_offset=bass.IndirectOffsetOnAxis(ap=seats[0:n, j, k:k + 1], axis=0),
                                             in_=staged[0:n, j, k, :], in_offset=None).then_inc(scattered, 16)

            def slot(h, layer, after, project, late, embed, route=(None, None, None)):
                at = place(late)
                par = parity_of(h, layer)
                pool.wait_ge(c_ready, h + 1)
                for i in range(GROUPS):
                    pool.wait_ge(scan_done, 16 * h + i + 1)
                    if not (early(h, 1) and i < 8):
                        pool.wait_ge(nsum_done, 4 * h + i // 4 - 1)
                    nc.gpsimd.tensor_tensor(hc[i % 8][:], state[i % 4][:], C[par][:], ALU.mult).then_inc(hc_done, 1)
                    if project and i == at["dt_lo"]:
                        low_dt(project[0])
                    if route[2] is not None and i in at["scatters"]:
                        scatter(route[2], scatter_half(h, layer), at["scatters"].index(i))

            run_slots(pool, slot)
            for k in range(CHUNKS):
                scatter(TILES - 3, 1, k)
            for t in (TILES - 2, TILES - 1):
                for j in range(TOP):
                    for k in range(CHUNKS):
                        scatter(t, j, k)
            def store_rows(b, m, n, before_):
                if before_ is not None:
                    pool.wait_ge(stored[b], before_)
                pool.wait_ge(goes_ready, n)
                nc.gpsimd.tensor_copy(goes_now[b][:], goes[:, bass.ds(m, 1)]).then_inc(goes_set, 1)
                pool.wait_ge(goes_set, n)
                pool.wait_ge(y_ready, n)
                if not isinstance(m, int):
                    nc.gpsimd.tensor_tensor(held[:], ident[0:1, 0:1], ident[0:1, 0:1], ALU.mult)
                nc.gpsimd.indirect_dma_start(out=results, out_offset=bass.IndirectOffsetOnAxis(ap=goes_now[b][:], axis=0),
                                             in_=ysb[b][:], in_offset=None, bounds_check=TOP * RESULT - 1,
                                             oob_is_err=False).then_inc(stored[b], 16)

            for b in range(2):
                store_rows(b, b, b + 1, None)
            with pool.Fori(1, BLOCKS // 2) as j:
                turns, nth = [pool.snap(2 * j), pool.snap(2 * j + 1), pool.snap(2 * j + 2)], pool.snap(16 * j)
                for b in range(2):
                    store_rows(b, turns[b], turns[b + 1], nth)

        @block.scalar
        def _(act):
            nc.scalar.preload_act_table_set("natural_log_exp_and_others")
            act.wait_ge(param_in, 16 * PARAM_DMAS)

            def z_rows(x, layer):
                act.wait_ge(wdt_done, x + 1)
                if not early(x, 1):
                    act.wait_ge(dt_done, x)
                nc.scalar.activation(zpre[:], bank(PRE), ACT.Identity, bias=bdt(layer)).then_inc(z_done, 1)

            def z_abs(x):
                act.wait_ge(z_done, x + 1)
                nc.scalar.activation(zexp[:], zpre[:], ACT.Abs).then_inc(abs_done, 1)

            def z_exp(x):
                act.wait_ge(abs_done, x + 1)
                nc.scalar.activation(zexp[:], zexp[:], ACT.Exp, scale=-1.0).then_inc(zexp_done, 1)

            def z_log(x):
                act.wait_ge(zexp_done, x + 1)
                nc.scalar.activation(zexp[:], zexp[:], ACT.Ln, bias=one).then_inc(zlog_done, 1)

            def b_rows(x, par, layer):
                act.wait_ge(wb_done, x + 1)
                if not early(x, 2):
                    act.wait_ge(b_done, 16 * (x - 1))
                nc.scalar.activation(B[par][:], bank(PRE), ACT.Identity, bias=bbr(layer)).then_inc(b_ready, 1)

            def c_rows(x, par, layer):
                act.wait_ge(wc_done, x + 1)
                if not early(x, 2):
                    act.wait_ge(hc_done, 16 * (x - 1))
                nc.scalar.activation(C[par][:], bank(PRE), ACT.Identity, bias=bcr(layer)).then_inc(c_ready, 1)

            def high_dt(x):
                act.wait_ge(dt_done, x + 1)
                if not early(x, 1):
                    act.wait_ge(s_in, 128 * x)
                if not early(x, 2):
                    act.wait_ge(exp_done, 16 * (x - 1))
                    act.wait_ge(b_done, 16 * (x - 1))
                nc.scalar.copy(dt_hi[:], dt[:]).then_inc(hi_done, 1)

            def high_dx(x):
                act.wait_ge(dx_done, x + 1)
                nc.scalar.copy(dx_hi[:], dx[:]).then_inc(hi_done, 1)

            def h_rows(t):
                act.wait_ge(tok_done, t + 1)
                nc.scalar.copy(tile_of(hT, t), bank(PRE)).then_inc(h_done, 1)

            def centred(t):
                act.wait_ge(cenm_done, t + 1)
                if not early(t, 1):
                    act.wait_ge(y0_done, t)
                nc.scalar.copy(cen[:], bank(PRE)).then_inc(cen_done, 1)

            def squared(t):
                act.wait_ge(cen_done, t + 1)
                nc.scalar.activation(sq[:], cen[:], ACT.Square).then_inc(sq_done, 1)

            def log_variance(t):
                act.wait_ge(var_done, t + 1)
                nc.scalar.activation(rstd[:], bank(PRE), ACT.Ln, bias=epsc).then_inc(ln_done, 1)

            def inverse_std(t):
                act.wait_ge(ln_done, t + 1)
                nc.scalar.activation(rstd[:], rstd[:], ACT.Exp, scale=-0.5).then_inc(rstd_done, 1)

            def relu(h):
                act.wait_ge(nsum_done, 4 * h + 4)
                nc.scalar.activation(act_y[:], bank(NSUM), ACT.Relu).then_inc(relu_done, 1)

            def lin_bias(h, layer):
                act.wait_ge(lin_done, h + 1)
                nc.scalar.activation((Y[1], lin1)[layer][:], bank(POST), ACT.Identity, bias=bln(layer)).then_inc(linb_done, 1)

            def residual(t):
                act.wait_ge(dec_done, t + 1)
                if not early(t, 1):
                    act.wait_ge(r_trh, t)
                nc.scalar.activation(h_s[:, 0:TOK], bank(POST), ACT.Identity, bias=bdec).then_inc(resid_done, 1)

            def route_centred(t, k=POST):
                act.wait_ge(r_cenm, t + 1)
                if not early(t, 1):
                    act.wait_ge(r_xn, t)
                nc.scalar.copy(rcen[:], bank(k)).then_inc(r_cen, 1)

            def route_squared(t):
                act.wait_ge(r_cen, t + 1)
                nc.scalar.activation(rsq[:], rcen[:], ACT.Square).then_inc(r_sq, 1)

            def route_log(t, k=POST):
                act.wait_ge(r_var, t + 1)
                nc.scalar.activation(rrstd[:], bank(k), ACT.Ln, bias=epsc).then_inc(r_ln, 1)

            def route_rstd(t):
                act.wait_ge(r_ln, t + 1)
                nc.scalar.activation(rrstd[:], rrstd[:], ACT.Exp, scale=-0.5).then_inc(r_rstd, 1)

            def route_exp(t):
                act.wait_ge(r_shift, t + 1)
                nc.scalar.activation(prob[:], prob[:], ACT.Exp).then_inc(r_pexp, 1)

            def route_htok(t):
                act.wait_ge(r_trh, t + 1)
                nc.scalar.copy(htok[:, bass.ds(t, 1), :].rearrange("p t n -> p (t n)"), bank(PRE, 512, CHUNK)).then_inc(r_htok, 1)

            def route_staged(t):
                act.wait_ge(r_trx, t + 1)
                if not early(t, 1):
                    act.wait_ge(scattered, 128 * t)
                for j in range(TOP):
                    nc.scalar.copy(staged[:, j, :, 0:CHANNELS],
                                   bank(PRE, 512, CHUNK).rearrange("p (k d) -> p k d", k=CHUNKS)).then_inc(r_staged, 1)

            def prepare(x, par, layer):
                z_rows(x, layer)
                b_rows(x, par, layer)
                z_abs(x)
                c_rows(x, par, layer)
                z_exp(x)
                z_log(x)
                high_dt(x)
                high_dx(x)

            h_rows(0)
            centred(0)
            squared(0)
            log_variance(0)
            inverse_std(0)
            prepare(0, 0, 0)

            def slot(h, layer, after, project, late, embed, route=(None, None, None)):
                at = place(late)
                par = parity_of(h, layer)
                for i in range(GROUPS):
                    act.wait_ge(rep_dt, 16 * h + i + 1)
                    if not (early(h, 1) and i < 4):
                        act.wait_ge(scan_done, 16 * h + i - 3)
                    nc.scalar.activation(decay[i % 4][:, :, 1:LENGTH],
                                         bank(DT + i % 2).rearrange("p (b t) -> p b t", b=PER_TILE)[:, :, 1:LENGTH],
                                         ACT.Exp, scale=acol[:, layer, group(i):group(i) + 1]).then_inc(exp_done, 1)
                    if after:
                        t, l = after
                        if i == at["relu"]:
                            relu(h - 1)
                        if i == at["lin_b"]:
                            lin_bias(h - 1, l)
                        if i == at["resid"] and l == 1:
                            residual(t)
                    if route[0] is not None:
                        if i == at["r_cen"]:
                            route_centred(route[0])
                        if i == at["r_sq"]:
                            route_squared(route[0])
                    if route[1] is not None:
                        if i == at["r_ln"]:
                            route_log(route[1])
                        if i == at["r_rstd"]:
                            route_rstd(route[1])
                        if i == at["r_pexp"]:
                            route_exp(route[1])
                        if i == at["r_htok"]:
                            route_htok(route[1])
                        if i == at["r_staged"]:
                            route_staged(route[1])
                    if embed is not None:
                        if i == at["h"]:
                            h_rows(embed)
                        if i == at["cen"]:
                            centred(embed)
                        if i == at["sq"]:
                            squared(embed)
                        if i == at["lnv"]:
                            log_variance(embed)
                        if i == at["rstd"]:
                            inverse_std(embed)
                    if project:
                        x, l, _ = project
                        if i == at["z"]:
                            z_rows(x, l)
                        if i == at["b"]:
                            b_rows(x, 1 - par, l)
                        if i == at["abs"]:
                            z_abs(x)
                        if i == at["exp"]:
                            z_exp(x)
                        if i == at["ln"]:
                            z_log(x)
                        if i == at["c"]:
                            c_rows(x, 1 - par, l)
                        if i == at["dt_hi"]:
                            high_dt(x)
                        if i == at["dx_hi"]:
                            high_dx(x)

            run_slots(act, slot)
            route_log(TILES - 2)
            route_rstd(TILES - 2)
            relu(SLOTS - 1)
            route_exp(TILES - 2)
            route_htok(TILES - 2)
            route_staged(TILES - 2)
            lin_bias(SLOTS - 1, 1)
            residual(TILES - 1)
            route_centred(TILES - 1)
            route_squared(TILES - 1)
            route_log(TILES - 1)
            route_rstd(TILES - 1)
            route_exp(TILES - 1)
            route_htok(TILES - 1)
            route_staged(TILES - 1)

            def copy_x(b, n, first=False):
                act.wait_ge(turned, n)
                nc.scalar.copy(xT[b][:], bank(6 + b, 128)).then_inc(xT_ready, 1)

            def relus(b, n):
                act.wait_ge(up_done, n)
                for f in (0, 1):
                    ins = nc.scalar.activation(hid[b][:, f, :], up_out(b, f), ACT.Relu,
                                               bias=up_w[b][:, HIDDEN + f:HIDDEN + f + 1])
                ins.then_inc(relu_a, 1)

            def copy_up(m, b):
                e = act.value_load(table[0:1, 1, m:m + 1] if isinstance(m, int) else table[0:1, 1, bass.ds(m, 1)],
                                   min_val=0, max_val=EXPERTS - 1)
                if not early(m, 2):
                    act.wait_ge(relu_a, m - 1)
                    act.wait_ge(relu_v, m - 1)
                nc.scalar.copy(up_w[b][:], up_all[:, bass.ds(e, 1), :].rearrange("p e n -> p (e n)")).then_inc(up_copied, 1)

            act.wait_ge(moe_in, 32)
            act.wait_ge(t_ready, 1)
            copy_up(0, 0)
            copy_x(0, 1)
            copy_up(1, 1)
            relus(0, 1)
            copy_x(1, 2)

            def turn(m, b):
                copy_up(m + 1, 1 - b)
                relus(b, m + 1)
                copy_x(1 - b, m + 2)

            turn(1, 1)
            with act.Fori(1, BLOCKS // 2 - 1) as j:
                turn(2 * j, 0)
                turn(2 * j + 1, 1)
            turn(BLOCKS - 2, 0)
            relus(1, BLOCKS)

            with act.Fori(0, TILES) as t:
                nth = act.snap(t + 1)
                act.wait_ge(summed, nth)
                tile = out.rearrange("(t r) d -> t r d", t=TILES)[bass.ds(t, 1), :, :]
                act.dma_start(tile[:, 0:3 * CHUNK, :].rearrange("a (k p) d -> p (a k) d", k=3),
                              yb[:, bass.ds(t, 1), 0, 0:3, :].rearrange("p t k d -> p (t k) d")).then_inc(out_done, 16)
                act.dma_start(tile[:, 3 * CHUNK:TOK, :].rearrange("a p d -> p (a d)"),
                              yb[0:CHUNK_TOK[3], bass.ds(t, 1), 0, 3, :].rearrange("p t d -> p (t d)")).then_inc(out_done, 16)
            act.wait_ge(out_done, 16 * 2 * TILES)

        @block.vector
        def _(dve):
            nc.vector.memset(mean_w[:], 1.0 / CHANNELS).then_inc(consts, 1)
            for k in range(4):
                nc.vector.memset(decay[k][:, :, 0:1], 0.0).then_inc(consts, 1)
            nc.vector.memset(padding[:, 0:CHANNELS], 0.0).then_inc(pad_set, 1)
            nc.vector.memset(padding[:, CHANNELS:ROW].bitcast(i32), NOWHERE).then_inc(pad_set, 1)
            nc.vector.memset(h_s[:, TOK:CHUNKS * CHUNK], 0.0).then_inc(consts, 1)
            nc.vector.memset(xn[:, TOK:CHUNKS * CHUNK], 0.0).then_inc(consts, 1)
            nc.vector.memset(onesb[:], 1.0).then_inc(consts, 1)
            dve.wait_ge(param_in, 16 * PARAM_DMAS)
            nc.vector.tensor_copy(beforeb[:], before_in[:]).then_inc(consts, 1)
            nc.vector.tensor_copy(fill[:], region).then_inc(consts, 1)
            nc.vector.tensor_scalar(cen_w[:], ident[:], 1.0 / CHANNELS, None, ALU.subtract).then_inc(consts, 1)
            nc.vector.tensor_copy(spreadr[:], spread_in[:]).then_inc(consts, 1)
            for l in range(LAYERS):
                nc.vector.tensor_scalar(dskip[:, l, :], ident[:], dsk(l), None, ALU.mult).then_inc(consts, 1)
                for wide, narrow in ((wb, wb16), (wc, wc16)):
                    nc.vector.tensor_copy(wide[:, l, :, :],
                                          narrow[:, l, :].unsqueeze(2).to_broadcast([128, STATES, GCH])).then_inc(consts, 1)

            def normal(t, h):
                dve.wait_ge(rstd_done, t + 1)
                if h is not None:
                    dve.wait_ge(diag_done, h + 1)
                nc.vector.tensor_tensor(Y[0][:], cen[:], rstd[:], ALU.mult).then_inc(y0_done, 1)

            def step(x):
                dve.wait_ge(zlog_done, x + 1)
                if not early(x, 1):
                    dve.wait_ge(dtlo_done, x)
                nc.vector.scalar_tensor_tensor(out=dt[:], in0=zpre[:], scalar=0.0, in1=zexp[:], op0=ALU.max,
                                               op1=ALU.add).then_inc(dt_done, 1)

            def step_times_y(x, layer):
                dve.wait_ge(dt_done, x + 1)
                nc.vector.tensor_tensor(dx[:], dt[:], Y[layer][:], ALU.mult).then_inc(dx_done, 1)

            def low_dx(x):
                dve.wait_ge(hi_done, 2 * x + 2)
                if not early(x, 1):
                    dve.wait_ge(s_in, 128 * x)
                nc.vector.tensor_tensor(dx_lo[:], dx[:], dx_hi[:].bitcast(f32), ALU.subtract).then_inc(dxlo_done, 1)

            STEPS = 18

            def linker(t, n):
                count = [n]

                def link(ins):
                    count[0] += 1
                    ins.then_inc(r_step, 1)
                    dve.wait_ge(r_step, t * STEPS + count[0])
                return link

            def over_experts(a):
                return a.unsqueeze(2).to_broadcast(E3)

            def over_chunks(a):
                return a.unsqueeze(1).to_broadcast(E3)

            def route_norm(t):
                dve.wait_ge(r_rstd, t + 1)
                if not early(t, 1):
                    dve.wait_ge(r_trx, t)
                nc.vector.tensor_tensor(xn[:, 0:TOK], rcen[:], rrstd[:], ALU.mult).then_inc(r_xn, 1)

            def route_shift(t, k=POST):
                link = linker(t, 0)
                dve.wait_ge(r_logit, t + 1)
                lg = bank(k, CHUNKS * EXPERTS, CHUNK).rearrange("p (k e) -> p k e", k=CHUNKS)
                link(nc.vector.tensor_tensor(prob[:], lg, over_chunks(brr[0:CHUNK, :]), ALU.add))
                link(nc.vector.tensor_reduce(small_k[:], prob[:], AX.X, ALU.max))
                nc.vector.tensor_tensor(prob[:], prob[:], over_experts(small_k[:]), ALU.subtract).then_inc(r_shift, 1)

            def route_prob(t):
                link = linker(t, 2)
                dve.wait_ge(r_pexp, t + 1)
                link(nc.vector.tensor_reduce(small_k[:], prob[:], AX.X, ALU.add))
                link(nc.vector.reciprocal(small_k[:], small_k[:]))
                link(nc.vector.tensor_tensor(prob[:], prob[:], over_experts(small_k[:]), ALU.mult))

            def choose(link, j, of, n):
                link(nc.vector.tensor_reduce(top[:, j, :], of[:], AX.X, ALU.max))
                link(nc.vector.tensor_tensor(same[:], of[:], over_experts(top[:, j, :]), ALU.is_equal))
                link(nc.vector.tensor_tensor(same[:], same[:], over_chunks(first_of[0:CHUNK, :]), ALU.mult))
                link(nc.vector.tensor_reduce(key[:], same[:], AX.X, ALU.max))
                link(nc.vector.tensor_tensor(hot[j][:], over_chunks(first_of[0:CHUNK, :]), over_experts(key[:]), ALU.is_equal))

            def route_top1(t):
                link = linker(t, 5)
                choose(link, 0, prob, 5)

            def route_top2(t):
                link = linker(t, 10)
                link(nc.vector.scalar_tensor_tensor(out=left[:], in0=hot[0][:], scalar=-2.0, in1=prob[:], op0=ALU.mult, op1=ALU.add))
                choose(link, 1, left, 11)

            def route_mask(t):
                link = linker(t, 16)
                nc.vector.tensor_copy(gates[:, bass.ds(t, 1), :, :].rearrange("p t j k -> p (t j k)"),
                                      top[:].rearrange("p j k -> p (j k)"))
                link(nc.vector.tensor_tensor(same[:], hot[0][:], hot[1][:], ALU.add))
                if not early(t, 1):
                    dve.wait_ge(r_prefix, t)
                nc.vector.tensor_tensor(taken[:], same[:], over_experts(valid), ALU.mult).then_inc(r_mask, 1)

            def route_seats(t, k=POST):
                link = linker(t, 17)
                dve.wait_ge(r_prefix, t + 1)
                rank = bank(k, CHUNKS * EXPERTS, CHUNK).rearrange("p (k e) -> p k e", k=CHUNKS)
                link(nc.vector.tensor_tensor(seat[:], rank, over_chunks(fill[0:CHUNK, :]), ALU.add))
                total = psum[:, k * BANK + 64:k * BANK + 64 + EXPERTS]
                nc.vector.tensor_tensor(fill[:], fill[:], total, ALU.add)
                if not early(t, 1):
                    dve.wait_ge(scattered, 128 * t)
                for j in range(TOP):
                    ins = nc.vector.tensor_tensor((pick, same)[j][:], hot[j][:], seat[:], ALU.mult)
                ins.then_inc(r_pick, 1)
                dve.wait_ge(r_pick, t + 1)
                for j in range(TOP):
                    ins = nc.vector.tensor_reduce(seat_f[:, j, :], (pick, same)[j][:], AX.X, ALU.add)
                nc.vector.tensor_copy(staged[:, :, :, CHANNELS:ROW].bitcast(i32), plc[:].unsqueeze(3)).then_inc(r_places, 1)
                ins.then_inc(r_sum, 1)
                dve.wait_ge(r_sum, t + 1)
                nc.vector.tensor_copy(seats[:], seat_f[:]).then_inc(r_seats, 1)
                dve.wait_ge(r_places, t + 1)
                nc.vector.tensor_scalar(plc[:], plc[:], float(CHUNKS * CHUNK), None, ALU.add).then_inc(r_moved, 1)

            normal(0, None)
            step(0)
            step_times_y(0, 0)
            low_dx(0)

            def slot(h, layer, after, project, late, embed, route=(None, None, None)):
                at = place(late)
                par = parity_of(h, layer)

                def drive(i):
                    dve.wait_ge(rep_dx, 16 * h + i + 1)
                    nc.vector.tensor_tensor(bank(DX + i % 3), bank(DX + i % 3), B[par][:], ALU.mult).then_inc(b_done, 1)

                dve.wait_ge(b_ready, h + 1)
                drive(0)
                for i in range(GROUPS):
                    if i + 1 < GROUPS:
                        drive(i + 1)
                    dve.wait_ge(exp_done, 16 * h + i + 1)
                    dve.wait_ge(b_done, 16 * h + i + 1)
                    if not (early(h, 1) and i < 4):
                        dve.wait_ge(hc_done, 16 * h + i - 3)
                    nc.vector.tensor_tensor_scan(state[i % 4][:], decay[i % 4][:].rearrange("p b t -> p (b t)"),
                                                 bank(DX + i % 3), 0.0, ALU.mult, ALU.add).then_inc(scan_done, 1)
                    if embed is not None and i == at["normal"]:
                        normal(embed, h)
                    if project:
                        x, l, _ = project
                        if i == at["dt"]:
                            step(x)
                        if i == at["dx"]:
                            step_times_y(x, l)
                        if i == at["dx_lo"]:
                            low_dx(x)
                    if route[1] is not None:
                        t = route[1]
                        for name, job in (("r_xn", route_norm), ("r_shift", route_shift), ("r_prob", route_prob),
                                          ("r_top1", route_top1), ("r_top2", route_top2), ("r_mask", route_mask),
                                          ("r_seats", route_seats)):
                            if i == at[name]:
                                job(t)

            run_slots(dve, slot)
            for t in (TILES - 2, TILES - 1):
                for job in (route_norm, route_shift, route_prob, route_top1, route_top2, route_mask, route_seats):
                    job(t)

            count = [0]

            def link(ins):
                count[0] += 1
                ins.then_inc(t_step, 1)
                dve.wait_ge(t_step, count[0])

            nblk, upto, start, here, tmp = (a[:] for a in tab8)
            nc.vector.tensor_copy(ends[:], fill[:]).then_inc(pad_set, 1)
            link(nc.vector.tensor_tensor(nblk, fill[:], region, ALU.subtract))
            link(nc.vector.tensor_scalar(blocks_i[:], nblk, 127.0, None, ALU.add))
            link(nc.vector.tensor_scalar(blocks_i[:], blocks_i[:], 7, None, ALU.logical_shift_right))
            link(nc.vector.tensor_copy(nblk, blocks_i[:]))
            link(nc.vector.memset(here, 1.0))
            link(nc.vector.tensor_tensor_scan(upto, here, nblk, 0.0, ALU.mult, ALU.add))
            link(nc.vector.tensor_tensor(start, upto, nblk, ALU.subtract))
            link(nc.vector.tensor_scalar(here, start, number, None, ALU.is_le))
            link(nc.vector.tensor_scalar(nblk, upto, number, None, ALU.is_gt))
            link(nc.vector.tensor_tensor(here, here, nblk, ALU.mult))
            link(nc.vector.tensor_scalar(tmp, start, number, -128.0, ALU.subtract, ALU.mult))
            link(nc.vector.tensor_tensor(tmp, tmp, region, ALU.add))
            link(nc.vector.tensor_tensor(tmp, tmp, here, ALU.mult))
            link(nc.vector.tensor_reduce(tab[:, 0:1], tmp, AX.X, ALU.add))
            link(nc.vector.tensor_scalar(tab[:, 2:3], upto[:, 7:8], number, None, ALU.is_le))
            link(nc.vector.tensor_tensor(tab[:, 2:3], tab[:, 2:3], spare, ALU.mult))
            link(nc.vector.tensor_tensor(tab[:, 0:1], tab[:, 0:1], tab[:, 2:3], ALU.add))
            link(nc.vector.tensor_tensor(tmp, here, expert, ALU.mult))
            nc.vector.tensor_reduce(tab[:, 1:2], tmp, AX.X, ALU.add).then_inc(t_cols, 1)
            dve.wait_ge(t_rows, 1)
            nc.vector.tensor_copy(table[:].rearrange("a c m -> a (c m)"), bank(4, 2 * BLOCKS, 1)).then_inc(t_ready, 1)

            dve.wait_ge(moe_in, 32)
            dve.wait_ge(t_ready, 1)

            def copy_down(e, b):
                nc.vector.tensor_copy(down_w[b][:], down_all[:, bass.ds(e, 1), :].rearrange("p e n -> p (e n)")).then_inc(down_copied, 1)

            def copy_goes(m, q, nth):
                dve.wait_ge(xg_in[q], 16 * nth)
                nc.vector.tensor_copy(goes[:, bass.ds(m, 1)], xg[q][:, CHANNELS:ROW].bitcast(i32)).then_inc(goes_ready, 1)

            def relus(b, n):
                dve.wait_ge(up_done, n)
                for f in (2, 3):
                    ins = nc.vector.tensor_scalar(hid[b][:, f, :], up_out(b, f),
                                                  up_w[b][:, HIDDEN + f:HIDDEN + f + 1], 0.0, ALU.add, ALU.max)
                ins.then_inc(relu_v, 1)

            def finish(b, n, before_):
                dve.wait_ge(down_done, n)
                if before_ is not None:
                    dve.wait_ge(stored[b], 16 * before_)
                nc.vector.tensor_tensor(ysb[b][:], bank(4 + b, 128), down_w[b][:, HIDDEN:DOWN],
                                        ALU.add).then_inc(y_ready, 1)

            def expert_of(m):
                return dve.value_load(table[0:1, 1, bass.ds(m, 1)], min_val=0, max_val=EXPERTS - 1)

            def turn(m, q, nth, done_before, is_last=False):
                b, o = q % 2, 1 - q % 2
                relus(b, m + 1)
                if done_before is not None:
                    finish(o, m, None if early(done_before, 1) else done_before)
                if not is_last:
                    e = expert_of(m + 1)
                    copy_goes(m + 1, (q + 1) % 4, nth)
                    if not early(m, 1):
                        dve.wait_ge(y_ready, m)
                    copy_down(e, o)

            copy_down(expert_of(0), 0)
            copy_goes(0, 0, 1)
            turn(0, 0, 1, None)
            turn(1, 1, 1, 0)
            turn(2, 2, 1, 0)
            turn(3, 3, 2, 1)
            with dve.Fori(1, BLOCKS // 4) as j:
                for q in range(4):
                    turn(4 * j + q, q, j + 1 if q < 3 else j + 2, 2 * j + (-1, 0, 0, 1)[q])
            turn(BLOCKS - 2, 0, BLOCKS // 4 + 1, BLOCKS // 2 - 2)
            turn(BLOCKS - 1, 1, None, BLOCKS // 2 - 1, is_last=True)
            finish(1, BLOCKS, BLOCKS // 2 - 1)

            def combine(t, fetched, q):
                dve.wait_ge(yb_in[q], fetched)
                for choice in range(TOP):
                    if choice:
                        dve.wait_ge(half_sum, t + 1)
                    for k in range(CHUNKS):
                        first = yb[:, bass.ds(t, 1), 0, k, :].rearrange("p t d -> p (t d)")
                        before_ = first if choice else \
                            htok[:, bass.ds(t, 1), CHANNELS * k:CHANNELS * (k + 1)].rearrange("p t d -> p (t d)")
                        ins = nc.vector.scalar_tensor_tensor(
                            out=first, in0=yb[:, bass.ds(t, 1), choice, k, :].rearrange("p t d -> p (t d)"),
                            scalar=gates[:, bass.ds(t, 1), choice, k:k + 1].rearrange("p t k -> p (t k)"),
                            in1=before_, op0=ALU.mult, op1=ALU.add)
                    ins.then_inc(summed if choice else half_sum, 1)

            with dve.Fori(0, TILES // 4) as j:
                for q in range(4):
                    combine(4 * j + q, 32 * j + 32, q)

        @block.tensor
        def _(pe):
            pe.wait_ge(param_in, 16 * PARAM_DMAS)
            pe.wait_ge(consts, CONSTS)
            pe.wait_ge(tok_in, 32)

            def tokens(t, prepared):
                if prepared is not None:
                    pe.wait_ge(c_ready, prepared)
                nc.tensor.matmul(bank(PRE), wtok[:], rows[:].rearrange("p b t -> p (b t)")[:, bass.ds(t * TOK, TOK)],
                                 start=True, stop=False)
                nc.tensor.matmul(bank(PRE), ident[:], pos2[:].rearrange("p b t -> p (b t)"), start=False,
                                 stop=True).then_inc(tok_done, 1)

            def centre(t):
                pe.wait_ge(h_done, t + 1)
                nc.tensor.matmul(bank(PRE), cen_w[:], tile_of(hT, t), start=True, stop=True).then_inc(cenm_done, 1)

            def variance(t):
                pe.wait_ge(sq_done, t + 1)
                nc.tensor.matmul(bank(PRE), mean_w[:], sq[:], start=True, stop=True).then_inc(var_done, 1)

            def project_dt(x, layer, ready, embed=None, staged_tiles=None):
                if staged_tiles is not None and not early(staged_tiles, 1):
                    pe.wait_ge(r_staged, 2 * staged_tiles)
                if layer == 0:
                    pe.wait_ge(y0_done, ready)
                else:
                    pe.wait_ge(linb_done, ready)
                if not early(x, 1):
                    pe.wait_ge(c_ready, x)
                if embed is not None:
                    pe.wait_ge(ln_done, embed + 1)
                nc.tensor.matmul(bank(PRE), wdt[:, layer, :], Y[layer][:], start=True, stop=True).then_inc(wdt_done, 1)

            def project_b(x, layer):
                pe.wait_ge(z_done, x + 1)
                nc.tensor.matmul(bank(PRE), wb[:, layer, :, :].rearrange("p n j -> p (n j)"), Y[layer][:],
                                 start=True, stop=True).then_inc(wb_done, 1)

            def project_c(x, layer):
                pe.wait_ge(b_ready, x + 1)
                nc.tensor.matmul(bank(PRE), wc[:, layer, :, :].rearrange("p n j -> p (n j)"), Y[layer][:],
                                 start=True, stop=True).then_inc(wc_done, 1)

            def linear(h, layer, route=(None, None)):
                pe.wait_ge(relu_done, h + 1)
                if route[1] is not None:
                    pe.wait_ge(r_shift, route[1] + 1)
                if route[0] is not None and not early(route[0], 1):
                    pe.wait_ge(r_seats, route[0])
                nc.tensor.matmul(bank(POST), wlin[:, layer, :], act_y[:], start=True, stop=True).then_inc(lin_done, 1)

            def decode(h, t):
                pe.wait_ge(linb_done, h + 1)
                nc.tensor.matmul(bank(POST), wdec[:], lin1[:], start=True, stop=False)
                nc.tensor.matmul(bank(POST), ident[:], tile_of(hT, t), start=False, stop=True).then_inc(dec_done, 1)

            def skip_term(h, layer):
                if not early(h, 1):
                    pe.wait_ge(relu_done, h)
                for quad in range(4):
                    ins = nc.tensor.matmul(psum[32 * quad:32 * quad + 32, NSUM * BANK:NSUM * BANK + TOK],
                                           dskip[:, layer, 32 * quad:32 * quad + 32], Y[layer][:], start=True, stop=False)
                ins.then_inc(diag_done, 1)

            def sum_states(h, k):
                pe.wait_ge(hc_done, 16 * h + 4 * k + 4)
                for i in range(4 * k, 4 * k + 4):
                    quad = group(i) // 4
                    ins = nc.tensor.matmul(psum[32 * quad:32 * quad + 32, NSUM * BANK:NSUM * BANK + TOK],
                                           gath[:, group(i) % 4, :], hc[i % 8][:], start=False, stop=(k == 3))
                ins.then_inc(nsum_done, 1)

            def route_centre(t):
                pe.wait_ge(resid_done, t + 1)
                nc.tensor.matmul(bank(POST), cen_w[:], h_s[:, 0:TOK], start=True, stop=True).then_inc(r_cenm, 1)

            def route_variance(t):
                pe.wait_ge(r_sq, t + 1)
                nc.tensor.matmul(bank(POST), mean_w[:], rsq[:], start=True, stop=True).then_inc(r_var, 1)

            def route_logits(t):
                pe.wait_ge(r_xn, t + 1)
                for k in range(CHUNKS):
                    ins = nc.tensor.matmul(psum[0:CHUNK, POST * BANK + EXPERTS * k:POST * BANK + EXPERTS * (k + 1)],
                                           xn[:, CHUNK * k:CHUNK * (k + 1)], wr[:], start=True, stop=True)
                ins.then_inc(r_logit, 1)

            def route_turn_h(t, prepared=None):
                if prepared is not None:
                    pe.wait_ge(c_ready, prepared)
                for k in range(CHUNKS):
                    ins = nc.tensor.transpose(psum[0:CHUNK, PRE * BANK + 128 * k:PRE * BANK + 128 * (k + 1)],
                                              h_s[:, CHUNK * k:CHUNK * (k + 1)], ident[:])
                ins.then_inc(r_trh, 1)

            def route_turn_x(t):
                pe.wait_ge(r_xn, t + 1)
                pe.wait_ge(r_htok, t + 1)
                for k in range(CHUNKS):
                    ins = nc.tensor.transpose(psum[0:CHUNK, PRE * BANK + 128 * k:PRE * BANK + 128 * (k + 1)],
                                              xn[:, CHUNK * k:CHUNK * (k + 1)], ident[:])
                ins.then_inc(r_trx, 1)

            def route_prefix(t, h=None):
                pe.wait_ge(r_mask, t + 1)
                if h is not None:
                    pe.wait_ge(linb_done, h)
                at0 = POST * BANK
                for k in range(CHUNKS):
                    dst = psum[0:CHUNK, at0 + EXPERTS * k:at0 + EXPERTS * (k + 1)]
                    for q in range(k):
                        nc.tensor.matmul(dst, onesb[:, 0:CHUNK], taken[:, q, :], start=(q == 0), stop=False)
                    nc.tensor.matmul(dst, beforeb[:], taken[:, k, :], start=(k == 0), stop=True)
                for q in range(CHUNKS):
                    ins = nc.tensor.matmul(psum[:, at0 + 64:at0 + 64 + EXPERTS], onesb[:], taken[:, q, :], start=(q == 0),
                                           stop=(q == CHUNKS - 1))
                ins.then_inc(r_prefix, 1)

            tokens(0, None)
            centre(0)
            variance(0)
            project_dt(0, 0, 1)
            project_b(0, 0)
            project_c(0, 0)

            def slot(h, layer, after, project, late, embed, route=(None, None, None)):
                at = place(late)
                par = parity_of(h, layer)
                pe.wait_ge(s_in, 128 * (h + 1))
                for i in range(GROUPS):
                    g = group(i)
                    if not (early(h, 1) and i < 2):
                        pe.wait_ge(exp_done, 16 * h + i - 1)
                    nc.tensor.matmul(bank(DT + i % 2), spreadr[:, g % 8, :], S_dt[par][:, g // 8, :], start=True,
                                     stop=True).then_inc(rep_dt, 1)
                    if not (early(h, 1) and i < 3):
                        pe.wait_ge(scan_done, 16 * h + (i - 2 if i >= 3 else (0, -2, -1)[i]))
                    nc.tensor.matmul(bank(DX + i % 3), spreadr[:, g % 8, :], S_dx[par][:, g // 8, :], start=True,
                                     stop=True).then_inc(rep_dx, 1)
                    if after and i == at["sum3"]:
                        sum_states(h - 1, 3)
                    if i == at["diag"]:
                        skip_term(h, layer)
                    if after:
                        t, l = after
                        if i == at["lin"]:
                            linear(h - 1, l, route)
                        if i == at["dec"] and l == 1:
                            decode(h - 1, t)
                    if i in (7, 11, 15):
                        sum_states(h, i // 4 - 1)
                    if route[0] is not None and i == at["r_cenm"]:
                        route_centre(route[0])
                    if route[1] is not None:
                        for name, job in (("r_var", route_variance), ("r_logit", route_logits), ("r_trh", route_turn_h),
                                          ("r_trx", route_turn_x), ("r_prefix", route_prefix)):
                            if i == at[name]:
                                if job is route_turn_h:
                                    job(route[1], h + 1 if late else h + 2)
                                elif job is route_prefix:
                                    job(route[1], h)
                                else:
                                    job(route[1])
                    if embed is not None:
                        if i == at["tok"]:
                            tokens(embed, (h + 1 if late else h + 2))
                        if i == at["cenm"]:
                            centre(embed)
                        if i == at["var"]:
                            variance(embed)
                    if project:
                        x, l, ready = project
                        if i == at["wdt"]:
                            project_dt(x, l, ready, embed if late else None,
                                       route[1] + 1 if late and route[1] is not None else route[0])
                        if i == at["wb"]:
                            project_b(x, l)
                        if i == at["wc"]:
                            project_c(x, l)

            run_slots(pe, slot)
            route_variance(TILES - 2)
            sum_states(SLOTS - 1, 3)
            route_logits(TILES - 2)
            route_turn_h(TILES - 2)
            route_turn_x(TILES - 2)
            route_prefix(TILES - 2)
            pe.wait_ge(r_seats, TILES - 1)
            linear(SLOTS - 1, 1)
            decode(SLOTS - 1, TILES - 1)
            route_centre(TILES - 1)
            route_variance(TILES - 1)
            route_logits(TILES - 1)
            pe.wait_ge(r_staged, 2 * TILES - 2)
            route_turn_h(TILES - 1)
            route_turn_x(TILES - 1)
            route_prefix(TILES - 1)
            pe.wait_ge(t_cols, 1)
            for c in range(2):
                ins = nc.tensor.matmul(psum[0:1, 4 * BANK + c * BLOCKS:4 * BANK + (c + 1) * BLOCKS], tab[0:BLOCKS, c:c + 1],
                                       ident[0:BLOCKS, 0:BLOCKS], start=True, stop=True)
            ins.then_inc(t_rows, 1)

            def turn_x(q, nth, m):
                pe.wait_ge(xg_in[q], 16 * nth)
                nc.tensor.transpose(bank(6 + q % 2, 128), xg[q][:, 0:CHANNELS], ident[:]).then_inc(turned, 1)

            def up(b, m):
                pe.wait_ge(xT_ready, m + 1)
                pe.wait_ge(up_copied, m + 1)
                for f in range(FCH):
                    ins = nc.tensor.matmul(up_out(b, f),
                                           up_w[b][:, 128 * f:128 * (f + 1)], xT[b][:], start=True, stop=True)
                ins.then_inc(up_done, 1)

            def down(b, m):
                pe.wait_ge(relu_a, m + 1)
                pe.wait_ge(relu_v, m + 1)
                pe.wait_ge(down_copied, m + 1)
                for f in range(FCH):
                    ins = nc.tensor.matmul(bank(4 + b, 128), hid[b][:, f, :],
                                           down_w[b][:, 128 * f:128 * (f + 1)], start=(f == 0), stop=(f == FCH - 1))
                ins.then_inc(down_done, 1)

            turn_x(0, 1, 0)
            up(0, 0)
            turn_x(1, 1, 1)

            def turn(m, q, nth):
                up(q % 2, m)
                if nth is not None:
                    turn_x((q + 1) % 4, nth, m + 1)
                down(1 - q % 2, m - 1)

            turn(1, 1, 1)
            turn(2, 2, 1)
            turn(3, 3, 2)
            with pe.Fori(1, BLOCKS // 4) as j:
                for q in range(4):
                    turn(4 * j + q, q, j + 1 if q < 3 else j + 2)
            turn(BLOCKS - 2, 0, BLOCKS // 4 + 1)
            turn(BLOCKS - 1, 1, None)
            down(1, BLOCKS - 1)


def kernel(**inputs):
    import concourse.bacc as bacc
    from concourse.bass_utils import run_bass_kernel_spmd

    g = {k: np.asarray(v) for k, v in inputs.items()}
    c = np.ascontiguousarray
    at = lambda n: g["L0_attn_" + n]
    fn = lambda n: g["L0_ffn_" + n]
    samples = (LENGTH + 1) * STRIDE
    cols = [at("bdt").T, np.repeat(at("bB"), GCH, axis=1).T, np.repeat(at("bC"), GCH, axis=1).T, at("D_skip").T, at("blin").T,
            at("bdec")[:, None], np.full((128, 1), EPS, np.float32), np.zeros((128, 1), np.float32), np.ones((128, 1), np.float32)]
    p = np.arange(128)
    spread = np.zeros((128, 8, 128), np.float32)
    gather = np.zeros((128, 4, 32), np.float32)
    for r in range(8):
        spread[:, r, :] = (p[:, None] % 64) == 8 * r + p[None, :] % 8
    for r in range(4):
        gather[:, r, :] = p[None, :32] == 8 * r + p[:, None] % 8
    before = np.triu(np.ones((CHUNK, CHUNK), np.float32), 1)
    small = np.zeros((128, 6 * EXPERTS), np.float32)
    small[:, 0:8] = EXPERTS - np.arange(EXPERTS)
    small[:, 8:16] = CAP * np.arange(EXPERTS)
    small[:, 16:20] = p[:, None] < np.array(CHUNK_TOK)
    small[:, 20] = p
    small[:, 21] = SPARE + 128 * np.maximum(p - FEWEST, 0)
    small[:, 24:32] = np.arange(EXPERTS)
    places = (RESULT * np.arange(TOP)[:, None] + CHUNK * np.arange(CHUNKS)[None, :])[None] + p[:CHUNK, None, None]
    arrays = {
        "x_rows": g["x"][:, :samples, 0].reshape(SEQS, LENGTH + 1, STRIDE).transpose(2, 0, 1),
        "w_tok": g["L0_tok_W"].T,
        "pos": g["L0_tok_pos_embed"][0, :LENGTH].T,
        "a_cols": at("A").reshape(LAYERS, GROUPS, GCH, STATES).transpose(3, 2, 0, 1).reshape(128, LAYERS, GROUPS),
        "w_dt": at("Wdt").transpose(1, 0, 2), "w_b": at("WB").transpose(1, 0, 2), "w_c": at("WC").transpose(1, 0, 2),
        "w_lin": at("Wlin").transpose(1, 0, 2), "w_dec": at("Wdec"),
        "vecs": np.concatenate(cols, axis=1),
        "w_r": fn("Wr"), "b_r": np.broadcast_to(fn("br"), (128, EXPERTS)),
        "w_up": np.concatenate([fn("W1").transpose(1, 0, 2), fn("b1").reshape(EXPERTS, FCH, 128).transpose(2, 0, 1)], axis=2),
        "w_down": np.concatenate([fn("W2").reshape(EXPERTS, FCH, 128, 128).transpose(2, 0, 1, 3).reshape(128, EXPERTS, HIDDEN),
                                  np.broadcast_to(fn("b2"), (128, EXPERTS, CHANNELS))], axis=2),
        "spread": spread, "gather": gather, "eye": np.eye(128, dtype=np.float32), "before": before,
        "small": small, "places": places.astype(np.float32),
    }
    arrays = {k: c(v) for k, v in arrays.items()}
    nc = bacc.Bacc("TRN2", target_bir_lowering=False, num_devices=1)
    args = [nc.dram_tensor(k, v.shape, mybir.dt.from_np(v.dtype), kind="ExternalInput").ap() for k, v in arrays.items()]
    out = nc.dram_tensor("out", (TOKENS, CHANNELS), mybir.dt.float32, kind="ExternalOutput").ap()
    audio_tower(nc, *args, out)
    r = run_bass_kernel_spmd(nc, [arrays], core_ids=[0])
    return r.results[0]["out"].reshape(SEQS, LENGTH, CHANNELS)
```

```python
import numpy as np
import concourse.bass as bass
from concourse import mybir
from contextlib import ExitStack

SEQS, LENGTH, CHANNELS, STATES, LAYERS = 16, 249, 128, 16, 2
PATCH, STRIDE = 64, 32
EXPERTS, HIDDEN, TOP = 8, 512, 2
PER_TILE = 2
TOK = PER_TILE * LENGTH
TILES = SEQS // PER_TILE
TOKENS = SEQS * LENGTH
SLOTS = TILES * LAYERS
GROUPS = CHANNELS // (128 // STATES)
GCH = CHANNELS // GROUPS
BANK = 512
CHUNK = 125
CHUNKS = 4
CHUNK_TOK = [125, 125, 125, TOK - 3 * CHUNK]
FCH = HIDDEN // 128
EPS = 1e-5
CAP = -(-TOKENS // 128) * 128 + 128
BLOCKS = (TOKENS * TOP) // 128 + EXPERTS
SPARE = EXPERTS * CAP
FEWEST = -(-TOKENS * TOP // 128)
EARLY = 36
assert EARLY % 4 == 0 and EARLY * 128 <= (TOKENS - 2 * TOK) * TOP - EXPERTS * 127
QUEUE_ROWS = SPARE + (BLOCKS - FEWEST) * 128
ROW = CHANNELS + 1
RESULT = TILES * CHUNKS * CHUNK
NOWHERE = 1 << 20
UP, DOWN = HIDDEN + FCH, HIDDEN + CHANNELS


def audio_tower(nc, x_rows, w_tok, pos, a_cols, w_dt, w_b, w_c, w_lin, w_dec, vecs, w_r, b_r, w_up, w_down,
                spread, gather, eye, before, small, places, out):
    f32, f32r, bf16, i32 = mybir.dt.float32, mybir.dt.float32r, mybir.dt.bfloat16, mybir.dt.int32
    queue = nc.dram_tensor("queue", (QUEUE_ROWS, ROW), f32, kind="Internal").ap()
    results = nc.dram_tensor("results", (TOP * RESULT, CHANNELS), f32, kind="Internal").ap()
    ALU, ACT, AX = mybir.AluOpType, mybir.ActivationFunctionType, mybir.AxisListType

    with ExitStack() as ctx:
        def sb(name, shape, dt=f32):
            return ctx.enter_context(nc.sbuf_tensor(name, shape, dt))

        def sem(name):
            return ctx.enter_context(nc.semaphore(name))

        rows = sb("rows", [PATCH, SEQS, LENGTH])
        wtok = sb("wtok", [PATCH, CHANNELS])
        pos2 = sb("pos2", [128, PER_TILE, LENGTH])
        acol = sb("acol", [128, LAYERS, GROUPS])
        wdt = sb("wdt", [128, LAYERS, 128])
        wb16 = sb("wb16", [128, LAYERS, STATES])
        wc16 = sb("wc16", [128, LAYERS, STATES])
        wb = sb("wb", [128, LAYERS, STATES, GCH])
        wc = sb("wc", [128, LAYERS, STATES, GCH])
        wlin = sb("wlin", [128, LAYERS, 128])
        wdec = sb("wdec", [128, 128])
        NV = 14
        vec = sb("vec", [128, NV])
        bdt, bbr, bcr, dsk, bln = (lambda l, k=k: vec[:, 2 * k + l:2 * k + l + 1] for k in range(5))
        bdec, epsc, zero, one = (vec[:, 10 + k:11 + k] for k in range(4))
        spread_in = sb("spread_in", [128, 8, 128])
        spreadr = sb("spreadr", [128, 8, 128], f32r)
        gath = sb("gath", [128, 4, 32])
        mean_w = sb("mean_w", [128, 128])
        ident = sb("ident", [128, 128])
        wr = sb("wr", [128, EXPERTS])
        brr = sb("brr", [128, EXPERTS])
        moe_all = sb("moe_all", [128, EXPERTS * (UP + DOWN)])
        up_all = moe_all[:, 0:EXPERTS * UP].rearrange("p (e n) -> p e n", e=EXPERTS)
        down_all = moe_all[:, EXPERTS * UP:].rearrange("p (e n) -> p e n", e=EXPERTS)
        before_in = sb("before_in", [CHUNK, CHUNK])
        beforeb = sb("beforeb", [CHUNK, CHUNK], bf16)
        onesb = sb("onesb", [CHUNK, 128], bf16)
        sml = sb("sml", [128, 6 * EXPERTS])
        first_of = sml[:, 0:8]
        region = sml[:, 8:16]
        valid = sml[0:CHUNK, 16:20]
        number = sml[:, 20:21]
        spare = sml[:, 21:22]
        expert = sml[:, 24:32]
        plc = sb("plc", [CHUNK, TOP, CHUNKS])

        hT = sb("hT", [128, TILES * TOK])
        Y = [sb(f"Y{l}", [128, TOK]) for l in range(LAYERS)]
        B = [sb(f"B{p}", [128, TOK]) for p in range(2)]
        C = [sb(f"C{p}", [128, TOK]) for p in range(2)]
        S_dt = [sb(f"S_dt{p}", [128, 2, TOK], f32r) for p in range(2)]
        S_dx = [sb(f"S_dx{p}", [128, 2, TOK], f32r) for p in range(2)]
        decay = [sb(f"decay{k}", [128, PER_TILE, LENGTH]) for k in range(4)]
        state = [sb(f"state{k}", [128, TOK]) for k in range(4)]
        hc_all = sb("hc_all", [128, 8 * TOK])
        hc = [hc_all[:, k * TOK:(k + 1) * TOK] for k in range(8)]
        cen_w = sb("cen_w", [128, 128])
        dskip = sb("dskip", [128, LAYERS, 128])
        act_y = sb("act_y", [128, TOK])
        lin1 = sb("lin1", [128, TOK])
        zpre = sb("zpre", [128, TOK])
        zexp = sb("zexp", [128, TOK])
        dt = sb("dt", [128, TOK])
        dx = sb("dx", [128, TOK])
        dt_hi, dt_lo, dx_hi, dx_lo = (sb(n, [128, TOK], f32r) for n in ("dt_hi", "dt_lo", "dx_hi", "dx_lo"))
        cen = sb("cen", [128, TOK])
        sq = sb("sq", [128, TOK])
        rstd = sb("rstd", [128, TOK])
        h_s = sb("h_s", [128, CHUNKS * CHUNK])
        rcen = sb("rcen", [128, TOK])
        rsq = sb("rsq", [128, TOK])
        rrstd = sb("rrstd", [128, TOK])
        xn = sb("xn", [128, CHUNKS * CHUNK])
        E3 = [CHUNK, CHUNKS, EXPERTS]
        prob = sb("prob", E3)
        small_k = sb("small_k", [CHUNK, CHUNKS])
        top = sb("top", [CHUNK, TOP, CHUNKS])
        key = sb("key", [CHUNK, CHUNKS])
        same = sb("same", E3)
        hot = [sb(f"hot{j}", E3) for j in range(TOP)]
        left = sb("left", E3)
        taken = sb("taken", E3, bf16)
        fill = sb("fill", [128, EXPERTS])
        seat = sb("seat", E3)
        pick = sb("pick", E3)
        seat_f = sb("seat_f", [CHUNK, TOP, CHUNKS])
        seats = sb("seats", [CHUNK, TOP, CHUNKS], i32)
        staged = sb("staged", [CHUNK, TOP, CHUNKS, ROW])
        gates = sb("gates", [CHUNK, TILES, TOP, CHUNKS])
        htok = sb("htok", [CHUNK, TILES, CHUNKS * CHANNELS])
        padding = sb("padding", [128, ROW])
        ends = sb("ends", [128, EXPERTS], i32)
        tab8 = [sb(f"tab8{k}", [128, EXPERTS]) for k in range(7)]
        blocks_i = sb("blocks_i", [128, EXPERTS], i32)
        tab = sb("tab", [128, 3])
        table = sb("table", [1, 2, BLOCKS], i32)
        xg = [sb(f"xg{b}", [128, ROW]) for b in range(4)]
        goes = sb("goes", [128, BLOCKS], i32)
        held = sb("held", [1, 1])
        goes_now = [sb(f"goes_now{b}", [128, 1], i32) for b in range(2)]

        def lay(store, at, n, parts=128):
            return [store[0:parts, at + b * n:at + (b + 1) * n] for b in range(2)]

        xT = lay(hT, 0, 128)
        ysb = lay(hT, 256, CHANNELS)
        up_w = lay(hc_all, 0, UP)
        down_w = lay(hc_all, 2 * UP, DOWN)
        hid = [v.rearrange("p (f m) -> p f m", f=FCH) for v in lay(hc_all, 2 * (UP + DOWN), FCH * 128)]
        yb = moe_all[0:CHUNK, 0:TILES * TOP * CHUNKS * CHANNELS].rearrange("p (t j k d) -> p t j k d", t=TILES, j=TOP, k=CHUNKS)

        psum = ctx.enter_context(nc.psum_tensor("psum", [128, 8 * BANK], f32))

        def bank(k, n=TOK, p=128):
            return psum[0:p, k * BANK:k * BANK + n]

        def up_out(b, f):
            at = (2 * b + f // 2) * BANK + 128 * (f % 2)
            return psum[:, at:at + 128]

        DT, DX, NSUM, POST, PRE = 0, 2, 5, 6, 7

        param_in, tok_in, moe_in = sem("param_in"), sem("tok_in"), sem("moe_in")
        embed_in, centre_set = sem("embed_in"), sem("centre_set")
        consts = sem("consts")
        rep_dt, rep_dx = sem("rep_dt"), sem("rep_dx")
        exp_done, b_done, scan_done = sem("exp_done"), sem("b_done"), sem("scan_done")
        hc_done, nsum_done = sem("hc_done"), sem("nsum_done")
        diag_done, abs_done, zexp_done, zlog_done = (sem(n) for n in ("diag_done", "abs_done", "zexp_done", "zlog_done"))
        relu_done, lin_done, linb_done = sem("relu_done"), sem("lin_done"), sem("linb_done")
        dec_done, resid_done = sem("dec_done"), sem("resid_done")
        tok_done, h_done, cenm_done, cen_done = sem("tok_done"), sem("h_done"), sem("cenm_done"), sem("cen_done")
        sq_done, var_done, ln_done, rstd_done, y0_done = (sem(n) for n in ("sq_done", "var_done", "ln_done", "rstd_done", "y0_done"))
        wdt_done, z_done, dt_done, dx_done = (sem(n) for n in ("wdt_done", "z_done", "dt_done", "dx_done"))
        hi_done, dtlo_done, dxlo_done, s_in = sem("hi_done"), sem("dtlo_done"), sem("dxlo_done"), [sem(f"s_in{k}") for k in range(2)]
        wb_done, b_ready, wc_done, c_ready = (sem(n) for n in ("wb_done", "b_ready", "wc_done", "c_ready"))

        (r_cenm, r_cen, r_sq, r_var, r_ln, r_rstd, r_xn, r_logit, r_shift, r_pexp, r_step, r_mask, r_prefix, r_seats,
         r_trh, r_htok, r_trx, r_staged, r_places) = (sem("r_" + n) for n in (
             "cenm", "cen", "sq", "var", "ln", "rstd", "xn", "logit", "shift", "pexp", "step", "mask", "prefix", "seats",
             "trh", "htok", "trx", "staged", "places"))
        r_filled = sem("r_filled")
        r_pick, r_sum, r_moved = (sem("r_" + n) for n in ("pick", "sum", "moved"))
        scattered, spare_in, pad_set, padded = (sem(n) for n in ("scattered", "spare_in", "pad_set", "padded"))
        t_step, t_cols, t_rows, t_ready = (sem(n) for n in ("t_step", "t_cols", "t_rows", "t_ready"))
        xg_in = [sem(f"xg_in{b}") for b in range(4)]
        goes_set = sem("goes_set")
        turned, xT_ready, goes_ready, up_copied, down_copied = (
            sem(n) for n in ("turned", "xT_ready", "goes_ready", "up_copied", "down_copied"))
        up_done, relu_a, relu_v, down_done, y_ready = (sem(n) for n in ("up_done", "relu_a", "relu_v", "down_done", "y_ready"))
        stored = [sem(f"stored{b}") for b in range(2)]
        yb_in = [sem(f"yb_in{t}") for t in range(TILES)]
        half_sum, summed, half_sum_p, summed_p = (sem(n) for n in ("half_sum", "summed", "half_sum_p", "summed_p"))
        out_done = sem("out_done")

        block = ctx.enter_context(nc.Block())

        def run_slots(engine, slot):
            def pair(t, a, b, c):
                slot(2 * t - 1, layer=0, after=(t - 2, 1), project=(2 * t, 1, 2 * t - 2), embed=t + 1 if a else None,
                     route=(t - 2, None, t - 3 if b else None, t - 3 if b else None))
                if c:
                    slot(2 * t, layer=1, after=(t, 0), project=(2 * t + 1, 0, t + 2), embed=None,
                         route=(None, t - 2, t - 3 if b else None, None))

            slot(0, layer=0, after=None, project=(1, 0, 2), embed=1)
            slot(1, layer=0, after=(0, 0), project=(2, 1, 1), embed=2)
            slot(2, layer=1, after=(1, 0), project=(3, 0, 3), embed=None)
            pair(2, True, False, True)
            with engine.Fori(3, TILES - 1) as t:
                pair(t, True, True, True)
            pair(TILES - 1, False, True, False)
            h = 2 * TILES - 2
            slot(h, layer=1, after=(TILES - 1, 0), project=(h + 1, 1, h), embed=None,
                 route=(None, TILES - 3, TILES - 4, None))
            slot(h + 1, layer=1, after=(TILES - 2, 1), project=None, embed=None,
                 route=(TILES - 2, TILES - 2, TILES - 3, TILES - 3))

        def parity_of(h, layer):
            return h % 2 if isinstance(h, int) else 1 - layer

        def group(i):
            return (i % 4) * 4 + i // 4

        def scatter_half(h, layer):
            return 1 - parity_of(h, layer)

        def tile_of(tensor, t):
            return tensor[:, bass.ds(t * TOK, TOK)]

        def early(x, n):
            return isinstance(x, int) and x < n

        def place(h, layer):
            h = h if isinstance(h, int) else None
            first, second, before_last, last = (h == k for k in (0, 1, SLOTS - 2, SLOTS - 1))

            def project(o):
                return dict(wdt=o, z=o + 1, abs=o + 2, wb=o + 3, exp=o + 3, b=o + 3, ln=o + 4, dt=o + 4, wc=o + 5, c=o + 5,
                            dx=o + 5, dt_hi=o + 6, dt_lo=o + 6, dx_hi=o + 7, dx_lo=o + 7)

            at = dict(sum0=8, sum1=12, sum2=1, sum3=4, relu=5, diag=7, lin=9, lin_b=10, dec=11, resid=12,
                      tok=7, h=8, cenm=10, cen=10, sq=11, var=13, lnv=13, rstd=14, normal=13,
                      r_cenm=14, r_cen=15, r_sq=15, r_var=1, r_ln=2, r_rstd=3, r_xn=3, r_logit=6, r_pexp=9, r_trh=10, r_htok=11,
                      r_trx=13, r_staged=14, r_prefix=3,
                      r_chain={**{n: 5.5 + n / 2 for n in range(3)}, **{n: 8 + (n - 3) / 2 for n in range(3, 19)}},
                      r_seat_chain={n: 4 + (n - 19) / 2 for n in range(19, 24)},
                      scatters=(7, 9, 11, 13) if layer == 0 else (0, 2, 4, 6), **project(0))
            if first:
                at.update(diag=0, tok=None, h=None, cenm=None, cen=None, sq=None, var=None, lnv=None, rstd=None, normal=0,
                          **project(2))
            if second or before_last:
                at.update(sum2=0, sum3=2, relu=2, lin=3, lin_b=3, diag=3, wdt=4, z=4, abs=5, wb=5, exp=6, b=6, ln=7, dt=6, wc=7,
                          c=8, dx=7, dt_hi=9, dt_lo=8, dx_hi=10, dx_lo=9,
                          tok=9, h=10, cenm=11, cen=11, sq=12, var=13, lnv=14, rstd=15, normal=14,
                          r_trh=0, r_htok=1, r_ln=1, r_rstd=2)
            if h == 2:
                at.update(project(2))
            if last:
                at.update(sum3=2, relu=3, diag=5, lin=6, lin_b=7, dec=8, resid=9, r_cenm=10, r_cen=10, r_sq=11, r_var=12, r_ln=13,
                          r_rstd=14, r_xn=14, r_trh=11, r_htok=12, r_logit=None, r_pexp=None, r_trx=None, r_staged=None,
                          r_chain={}, scatters=(5, 7, 9, 11))
            return at

        POOL_TILES = [1, 4]
        DVE_TILES = [t for t in range(TILES) if t not in POOL_TILES]
        PARAM_DMAS = 15
        CONSTS = 4 + 3 + 3 + LAYERS * 3

        @block.sync
        def _(sp):
            for dst, src in ((wtok[:], w_tok), (ident[:], eye), (pos2[:, 0, :], pos), (pos2[:, 1, :], pos)):
                sp.dma_start(dst, src).then_inc(embed_in, 16)
            for dst, src in ((wdt[:], w_dt), (vec[:], vecs), (wb16[:], w_b), (wc16[:], w_c),
                             (acol[:], a_cols), (spread_in[:], spread),
                             (gath[:], gather), (wlin[:], w_lin), (wdec[:], w_dec), (before_in[:], before),
                             (wr[:], w_r), (brr[:], b_r), (sml[:], small), (plc[:, 0, :], places[:, 0, :]),
                             (plc[:, 1, :], places[:, 1, :])):
                sp.dma_start(dst, src).then_inc(param_in, 16)
            sp.dma_start(up_all[:], w_up).then_inc(moe_in, 16)
            sp.dma_start(down_all[:], w_down).then_inc(moe_in, 16)
            sp.wait_ge(pad_set, 2)
            for k in range(BLOCKS - FEWEST):
                sp.dma_start(queue[SPARE + 128 * k:SPARE + 128 * k + 128, :], padding[:]).then_inc(spare_in, 16)

            for k in range(TOK, CHUNKS * CHUNK):
                none = results.rearrange("(a r) d -> a r d", r=CHUNKS * CHUNK)[:, k, :]
                sp.dma_start(none, padding[0:TOP * TILES, 0:CHANNELS]).then_inc(spare_in, 16)

            def place_split(x, par):
                first_hi, second_hi, lo_x = ((2 * x + 1, 2 * x + 2, x + 1) if isinstance(x, int) else
                                             (sp.snap(2 * x + 1), sp.snap(2 * x + 2), sp.snap(x + 1)))
                for n, (S, hi) in enumerate(((S_dt, dt_hi), (S_dx, dx_hi))):
                    sp.wait_ge(hi_done, (first_hi, second_hi)[n])
                    sp.dma_start(S[par][0:64, 0, :].bitcast(f32), hi[0:64, :].bitcast(f32)).then_inc(s_in[0], 16)
                    sp.dma_start(S[par][64:128, 1, :].bitcast(f32), hi[64:128, :].bitcast(f32)).then_inc(s_in[1], 16)
                sp.wait_ge(dtlo_done, lo_x)
                sp.dma_start(S_dt[par][64:128, 0, :].bitcast(f32), dt_lo[0:64, :].bitcast(f32)).then_inc(s_in[0], 16)
                sp.wait_ge(dxlo_done, lo_x)
                sp.dma_start(S_dx[par][64:128, 0, :].bitcast(f32), dx_lo[0:64, :].bitcast(f32)).then_inc(s_in[0], 16)
                sp.dma_start(S_dt[par][0:64, 1, :].bitcast(f32), dt_lo[64:128, :].bitcast(f32)).then_inc(s_in[1], 16)
                sp.dma_start(S_dx[par][0:64, 1, :].bitcast(f32), dx_lo[64:128, :].bitcast(f32)).then_inc(s_in[1], 16)

            place_split(0, 0)

            def slot(h, layer, after, project, embed, route=(None,) * 4):
                if project:
                    place_split(project[0], 1 - parity_of(h, layer))

            run_slots(sp, slot)

            def load(m, b, free, written=None):
                if isinstance(m, int):
                    row = sp.value_load(table[0:1, 0, m:m + 1], min_val=0, max_val=QUEUE_ROWS - 128)
                else:
                    row = sp.value_load(table[0:1, 0, bass.ds(m, 1)], min_val=0, max_val=QUEUE_ROWS - 128)
                if written is not None:
                    sp.wait_ge(scattered, written)
                if free is not None:
                    sp.wait_ge(turned, free)
                    sp.wait_ge(goes_ready, free)
                sp.dma_start(xg[b][:], queue[bass.ds(row, 128), :]).then_inc(xg_in[b], 16)

            sp.wait_ge(t_ready, 1)
            load(0, 0, None, 16 * (TILES - 2) * CHUNKS * TOP)
            for m in range(1, 4):
                load(m, m, None)

            def quad(j):
                free = [sp.snap(4 * j - 3 + b) for b in range(4)]
                for b in range(4):
                    load(4 * j + b, b, free[b])

            with sp.Fori(1, 4) as j:
                quad(j)
            sp.wait_ge(pad_set, 3)
            with sp.Fori(4, 4 + EXPERTS // 2) as j:
                quad(j)
                for e in range(2):
                    end = sp.value_load(ends[0:1, bass.ds(2 * j - 8 + e, 1)], min_val=0, max_val=SPARE - 128)
                    sp.dma_start(queue[bass.ds(end, 128), :], padding[:]).then_inc(padded, 16)
            with sp.Fori(4 + EXPERTS // 2, EARLY // 4) as j:
                quad(j)
            sp.wait_ge(padded, 16 * EXPERTS)
            sp.wait_ge(spare_in, 16 * (BLOCKS - FEWEST + CHUNKS * CHUNK - TOK))
            sp.wait_ge(scattered, 16 * TILES * CHUNKS * TOP)
            sp.wait_ge(t_ready, 2)
            with sp.Fori(EARLY // 4, BLOCKS // 4) as j:
                quad(j)
            for m in range(BLOCKS - 2, BLOCKS):
                load(m, m % 4, m - 3)

            for b in range(2):
                sp.wait_ge(stored[b], 16 * (BLOCKS // 2))
            for t in range(TILES):
                tile = results.rearrange("(j t r) d -> t j r d", j=TOP, t=TILES)
                for j in range(TOP):
                    src = tile[t, j, :, :].rearrange("(k p) d -> p k d", k=CHUNKS)
                    sp.dma_start(yb[:, t, j, :, :], src).then_inc(yb_in[t], 16)

        @block.gpsimd
        def _(pool):
            pool.dma_start(rows[0:STRIDE, :, :], x_rows[:, :, 0:LENGTH]).then_inc(tok_in, 16)
            pool.dma_start(rows[STRIDE:PATCH, :, :], x_rows[:, :, 1:LENGTH + 1]).then_inc(tok_in, 16)

            def scatter(t, j, k):
                if j == 0 and k == 0:
                    pool.wait_ge(r_seats, t + 1)
                    pool.wait_ge(r_staged, 2 * t + 2)
                    pool.wait_ge(r_places, t + 1)
                    if not isinstance(t, int):
                        nc.gpsimd.tensor_tensor(held[:], ident[0:1, 0:1], ident[0:1, 0:1], ALU.mult)
                n = CHUNK_TOK[k]
                nc.gpsimd.indirect_dma_start(out=queue, out_offset=bass.IndirectOffsetOnAxis(ap=seats[0:n, j, k:k + 1], axis=0),
                                             in_=staged[0:n, j, k, :], in_offset=None).then_inc(scattered, 16)

            def slot(h, layer, after, project, embed, route=(None,) * 4):
                at = place(h, layer)
                par = parity_of(h, layer)
                pool.wait_ge(c_ready, h + 1)
                for i in range(GROUPS):
                    pool.wait_ge(scan_done, 16 * h + i + 1)
                    if not (early(h, 1) and i < 8):
                        pool.wait_ge(nsum_done, 4 * h + i // 4 - 1)
                    nc.gpsimd.tensor_tensor(hc[i % 8][:], state[i % 4][:], C[par][:], ALU.mult).then_inc(hc_done, 1)
                    if route[2] is not None and i in at["scatters"]:
                        scatter(route[2], scatter_half(h, layer), at["scatters"].index(i))

            run_slots(pool, slot)
            for k in range(CHUNKS):
                scatter(TILES - 3, 1, k)
            for j in range(TOP):
                for k in range(CHUNKS):
                    scatter(TILES - 2, j, k)

            def store_rows(b, m, n, before_):
                if before_ is not None:
                    pool.wait_ge(stored[b], before_)
                pool.wait_ge(goes_ready, n)
                nc.gpsimd.tensor_copy(goes_now[b][:], goes[:, bass.ds(m, 1)]).then_inc(goes_set, 1)
                pool.wait_ge(goes_set, n)
                pool.wait_ge(y_ready, n)
                if not isinstance(m, int):
                    nc.gpsimd.tensor_tensor(held[:], ident[0:1, 0:1], ident[0:1, 0:1], ALU.mult)
                nc.gpsimd.indirect_dma_start(out=results, out_offset=bass.IndirectOffsetOnAxis(ap=goes_now[b][:], axis=0),
                                             in_=ysb[b][:], in_offset=None, bounds_check=TOP * RESULT - 1,
                                             oob_is_err=False).then_inc(stored[b], 16)

            for m in range(10 + 2 * TOP * CHUNKS):
                store_rows(m % 2, m, m + 1, 16 * (m // 2) if m >= 2 else None)
                if m >= 10 and m % 2 == 0:
                    n = (m - 10) // 2
                    scatter(TILES - 1, n // CHUNKS, n % CHUNKS)
            with pool.Fori(5 + TOP * CHUNKS, BLOCKS // 2) as j:
                turns, nth = [pool.snap(2 * j), pool.snap(2 * j + 1), pool.snap(2 * j + 2)], pool.snap(16 * j)
                for b in range(2):
                    store_rows(b, turns[b], turns[b + 1], nth)

            for n, t in enumerate(POOL_TILES):
                pool.wait_ge(yb_in[t], 32)
                for choice in range(TOP):
                    of = yb[:, t, choice, :, :]
                    gate = gates[:, t, choice, :].unsqueeze(2).to_broadcast([CHUNK, CHUNKS, CHANNELS])
                    nc.gpsimd.tensor_tensor(of, of, gate, ALU.mult).then_inc(half_sum_p, 1)
                pool.wait_ge(half_sum_p, 3 * n + 2)
                nc.gpsimd.tensor_tensor(yb[:, t, 0, :, :], yb[:, t, 0, :, :], yb[:, t, 1, :, :], ALU.add).then_inc(half_sum_p, 1)
                pool.wait_ge(half_sum_p, 3 * n + 3)
                nc.gpsimd.tensor_tensor(yb[:, t, 0, :, :], yb[:, t, 0, :, :],
                                        htok[:, t, :].rearrange("p (k d) -> p k d", k=CHUNKS), ALU.add).then_inc(summed_p, 1)

        @block.scalar
        def _(act):
            nc.scalar.preload_act_table_set("natural_log_exp_and_others")

            def z_rows(x, layer):
                act.wait_ge(wdt_done, x + 1)
                if not early(x, 1):
                    act.wait_ge(dt_done, x)
                nc.scalar.activation(zpre[:], bank(PRE), ACT.Identity, bias=bdt(layer)).then_inc(z_done, 1)

            def z_abs(x):
                act.wait_ge(z_done, x + 1)
                nc.scalar.activation(zexp[:], zpre[:], ACT.Abs).then_inc(abs_done, 1)

            def z_exp(x):
                act.wait_ge(abs_done, x + 1)
                nc.scalar.activation(zexp[:], zexp[:], ACT.Exp, scale=-1.0).then_inc(zexp_done, 1)

            def z_log(x):
                act.wait_ge(zexp_done, x + 1)
                nc.scalar.activation(zexp[:], zexp[:], ACT.Ln, bias=one).then_inc(zlog_done, 1)

            def b_rows(x, par, layer):
                act.wait_ge(wb_done, x + 1)
                if not early(x, 2):
                    act.wait_ge(b_done, 16 * (x - 1))
                nc.scalar.activation(B[par][:], bank(PRE), ACT.Identity, bias=bbr(layer)).then_inc(b_ready, 1)

            def c_rows(x, par, layer):
                act.wait_ge(wc_done, x + 1)
                if not early(x, 2):
                    act.wait_ge(hc_done, 16 * (x - 1))
                nc.scalar.activation(C[par][:], bank(PRE), ACT.Identity, bias=bcr(layer)).then_inc(c_ready, 1)

            def high_dt(x):
                act.wait_ge(dt_done, x + 1)
                if not early(x, 1):
                    for half in s_in:
                        act.wait_ge(half, 64 * x)
                if not early(x, 2):
                    act.wait_ge(exp_done, 16 * (x - 1))
                    act.wait_ge(b_done, 16 * (x - 1))
                nc.scalar.copy(dt_hi[:], dt[:]).then_inc(hi_done, 1)

            def high_dx(x):
                act.wait_ge(dx_done, x + 1)
                nc.scalar.copy(dx_hi[:], dx[:]).then_inc(hi_done, 1)

            def h_rows(t, k=PRE):
                act.wait_ge(tok_done, t + 1)
                nc.scalar.copy(tile_of(hT, t), bank(k)).then_inc(h_done, 1)

            def centred(t, k=PRE):
                act.wait_ge(cenm_done, t + 1)
                if not early(t, 1):
                    act.wait_ge(y0_done, t)
                nc.scalar.copy(cen[:], bank(k)).then_inc(cen_done, 1)

            def squared(t):
                act.wait_ge(cen_done, t + 1)
                nc.scalar.activation(sq[:], cen[:], ACT.Square).then_inc(sq_done, 1)

            def log_variance(t, k=PRE):
                act.wait_ge(var_done, t + 1)
                nc.scalar.activation(rstd[:], bank(k), ACT.Ln, bias=epsc).then_inc(ln_done, 1)

            def inverse_std(t):
                act.wait_ge(ln_done, t + 1)
                nc.scalar.activation(rstd[:], rstd[:], ACT.Exp, scale=-0.5).then_inc(rstd_done, 1)

            def relu(h):
                act.wait_ge(nsum_done, 4 * h + 4)
                nc.scalar.activation(act_y[:], bank(NSUM), ACT.Relu).then_inc(relu_done, 1)

            def lin_bias(h, layer, k=POST):
                act.wait_ge(lin_done, h + 1)
                nc.scalar.activation((Y[1], lin1)[layer][:], bank(k), ACT.Identity, bias=bln(layer)).then_inc(linb_done, 1)

            def residual(t, k=POST):
                act.wait_ge(dec_done, t + 1)
                if not early(t, 1):
                    act.wait_ge(r_trh, t)
                nc.scalar.activation(h_s[:, 0:TOK], bank(k), ACT.Identity, bias=bdec).then_inc(resid_done, 1)

            def route_centred(t, k=POST):
                act.wait_ge(r_cenm, t + 1)
                if not early(t, 1):
                    act.wait_ge(r_xn, t)
                nc.scalar.copy(rcen[:], bank(k)).then_inc(r_cen, 1)

            def route_squared(t):
                act.wait_ge(r_cen, t + 1)
                nc.scalar.activation(rsq[:], rcen[:], ACT.Square).then_inc(r_sq, 1)

            def route_log(t, k=POST):
                act.wait_ge(r_var, t + 1)
                nc.scalar.activation(rrstd[:], bank(k), ACT.Ln, bias=epsc).then_inc(r_ln, 1)

            def route_rstd(t):
                act.wait_ge(r_ln, t + 1)
                nc.scalar.activation(rrstd[:], rrstd[:], ACT.Exp, scale=-0.5).then_inc(r_rstd, 1)

            def route_exp(t):
                act.wait_ge(r_shift, t + 1)
                nc.scalar.activation(prob[:], prob[:], ACT.Exp).then_inc(r_pexp, 1)

            def route_htok(t, k=PRE):
                act.wait_ge(r_trh, t + 1)
                nc.scalar.copy(htok[:, bass.ds(t, 1), :].rearrange("p t n -> p (t n)"), bank(k, 512, CHUNK)).then_inc(r_htok, 1)

            def route_staged(t, at=PRE):
                act.wait_ge(r_trx, t + 1)
                if not early(t, 1):
                    act.wait_ge(scattered, 128 * t)
                for j in range(TOP):
                    nc.scalar.copy(staged[:, j, :, 0:CHANNELS],
                                   bank(at, 512, CHUNK).rearrange("p (k d) -> p k d", k=CHUNKS)).then_inc(r_staged, 1)

            h_rows(0)
            centred(0)
            squared(0)
            h_rows(1, POST)
            act.wait_ge(param_in, 16 * PARAM_DMAS)
            log_variance(0)
            inverse_std(0)
            z_rows(0, 0)
            centred(1, POST)
            squared(1)
            b_rows(0, 0, 0)
            z_abs(0)
            z_exp(0)
            z_log(0)
            c_rows(0, 0, 0)
            high_dt(0)
            high_dx(0)
            log_variance(1, POST)
            inverse_std(1)

            def slot(h, layer, after, project, embed, route=(None,) * 4):
                at = place(h, layer)
                par = parity_of(h, layer)
                for i in range(GROUPS):
                    act.wait_ge(rep_dt, 16 * h + i + 1)
                    if not (early(h, 1) and i < 4):
                        act.wait_ge(scan_done, 16 * h + i - 3)
                    nc.scalar.activation(decay[i % 4][:, :, 1:LENGTH],
                                         bank(DT + i % 2).rearrange("p (b t) -> p b t", b=PER_TILE)[:, :, 1:LENGTH],
                                         ACT.Exp, scale=acol[:, layer, group(i):group(i) + 1]).then_inc(exp_done, 1)
                    if after:
                        t, l = after
                        if i == at["relu"]:
                            relu(h - 1)
                        if i == at["lin_b"]:
                            lin_bias(h - 1, l)
                        if i == at["resid"] and l == 1:
                            residual(t)
                    if route[0] is not None:
                        if i == at["r_cen"]:
                            route_centred(route[0])
                        if i == at["r_sq"]:
                            route_squared(route[0])
                    if route[1] is not None:
                        if i == at["r_ln"]:
                            route_log(route[1])
                        if i == at["r_rstd"]:
                            route_rstd(route[1])
                        if i == at["r_pexp"]:
                            route_exp(route[1])
                        if i == at["r_htok"]:
                            route_htok(route[1])
                        if i == at["r_staged"]:
                            route_staged(route[1])
                    if embed is not None:
                        if i == at["h"]:
                            h_rows(embed)
                        if i == at["cen"]:
                            centred(embed)
                        if i == at["sq"]:
                            squared(embed)
                        if i == at["lnv"]:
                            log_variance(embed)
                        if i == at["rstd"]:
                            inverse_std(embed)
                    if project:
                        x, l, _ = project
                        if i == at["z"]:
                            z_rows(x, l)
                        if i == at["b"]:
                            b_rows(x, 1 - par, l)
                        if i == at["abs"]:
                            z_abs(x)
                        if i == at["exp"]:
                            z_exp(x)
                        if i == at["ln"]:
                            z_log(x)
                        if i == at["c"]:
                            c_rows(x, 1 - par, l)
                        if i == at["dt_hi"]:
                            high_dt(x)
                        if i == at["dx_hi"]:
                            high_dx(x)

            run_slots(act, slot)
            route_exp(TILES - 2)
            relu(SLOTS - 1)
            lin_bias(SLOTS - 1, 1, k=0)
            route_staged(TILES - 2)
            residual(TILES - 1, k=1)
            route_centred(TILES - 1, k=2)

            def copy_x(b, n):
                act.wait_ge(turned, n)
                nc.scalar.copy(xT[b][:], bank(POST, 128)).then_inc(xT_ready, 1)

            def relus(b, n):
                act.wait_ge(up_done, n)
                for f in (0, 1):
                    ins = nc.scalar.activation(hid[b][:, f, :], up_out(b, f), ACT.Relu,
                                               bias=up_w[b][:, HIDDEN + f:HIDDEN + f + 1])
                ins.then_inc(relu_a, 1)

            def copy_up(m, b):
                e = act.value_load(table[0:1, 1, m:m + 1] if isinstance(m, int) else table[0:1, 1, bass.ds(m, 1)],
                                   min_val=0, max_val=EXPERTS - 1)
                if not early(m, 2):
                    act.wait_ge(relu_a, m - 1)
                    act.wait_ge(relu_v, m - 1)
                nc.scalar.copy(up_w[b][:], up_all[:, bass.ds(e, 1), :].rearrange("p e n -> p (e n)")).then_inc(up_copied, 1)

            act.wait_ge(moe_in, 32)
            act.wait_ge(t_ready, 1)
            copy_up(0, 0)
            route_squared(TILES - 1)
            copy_x(0, 1)
            route_log(TILES - 1, k=3)
            route_rstd(TILES - 1)
            copy_up(1, 1)
            copy_x(1, 2)
            relus(0, 1)
            route_exp(TILES - 1)
            route_htok(TILES - 1, k=PRE)

            def turn(m, b):
                copy_up(m + 1, 1 - b)
                copy_x(1 - b, m + 2)
                relus(b, m + 1)

            turn(1, 1)
            turn(2, 0)
            turn(3, 1)
            route_staged(TILES - 1, at=PRE)
            with act.Fori(2, BLOCKS // 2 - 1) as j:
                turn(2 * j, 0)
                turn(2 * j + 1, 1)
            turn(BLOCKS - 2, 0)
            relus(1, BLOCKS)

            for t in range(TILES):
                if t in POOL_TILES:
                    act.wait_ge(summed_p, POOL_TILES.index(t) + 1)
                else:
                    act.wait_ge(summed, DVE_TILES.index(t) + 1)
                tile = out[t * TOK:(t + 1) * TOK, :]
                act.dma_start(tile[0:3 * CHUNK, :].rearrange("(k p) d -> p k d", k=3), yb[:, t, 0, 0:3, :]).then_inc(out_done, 16)
                act.dma_start(tile[3 * CHUNK:TOK, :], yb[0:CHUNK_TOK[3], t, 0, 3, :]).then_inc(out_done, 16)
            act.wait_ge(out_done, 16 * 2 * TILES)

        @block.vector
        def _(dve):
            nc.vector.memset(mean_w[:], 1.0 / CHANNELS).then_inc(centre_set, 1)
            for k in range(4):
                nc.vector.memset(decay[k][:, :, 0:1], 0.0).then_inc(consts, 1)
            nc.vector.memset(padding[:, 0:CHANNELS], 0.0).then_inc(pad_set, 1)
            nc.vector.memset(padding[:, CHANNELS:ROW].bitcast(i32), NOWHERE).then_inc(pad_set, 1)
            nc.vector.memset(h_s[:, TOK:CHUNKS * CHUNK], 0.0).then_inc(consts, 1)
            nc.vector.memset(xn[:, TOK:CHUNKS * CHUNK], 0.0).then_inc(consts, 1)
            nc.vector.memset(onesb[:], 1.0).then_inc(consts, 1)
            dve.wait_ge(embed_in, 16 * 4)
            nc.vector.tensor_scalar(cen_w[:], ident[:], 1.0 / CHANNELS, None, ALU.subtract).then_inc(centre_set, 1)
            dve.wait_ge(param_in, 16 * PARAM_DMAS)
            nc.vector.tensor_copy(beforeb[:], before_in[:]).then_inc(consts, 1)
            nc.vector.tensor_copy(fill[:], region).then_inc(consts, 1)
            nc.vector.tensor_copy(spreadr[:], spread_in[:]).then_inc(consts, 1)
            for l in range(LAYERS):
                nc.vector.tensor_scalar(dskip[:, l, :], ident[:], dsk(l), None, ALU.mult).then_inc(consts, 1)
                for wide, narrow in ((wb, wb16), (wc, wc16)):
                    nc.vector.tensor_copy(wide[:, l, :, :],
                                          narrow[:, l, :].unsqueeze(2).to_broadcast([128, STATES, GCH])).then_inc(consts, 1)

            def normal(t, h):
                dve.wait_ge(rstd_done, t + 1)
                if h is not None:
                    dve.wait_ge(diag_done, h + 1)
                nc.vector.tensor_tensor(Y[0][:], cen[:], rstd[:], ALU.mult).then_inc(y0_done, 1)

            def step(x):
                dve.wait_ge(zlog_done, x + 1)
                if not early(x, 1):
                    dve.wait_ge(dtlo_done, x)
                nc.vector.scalar_tensor_tensor(out=dt[:], in0=zpre[:], scalar=0.0, in1=zexp[:], op0=ALU.max,
                                               op1=ALU.add).then_inc(dt_done, 1)

            def step_times_y(x, layer):
                dve.wait_ge(dt_done, x + 1)
                nc.vector.tensor_tensor(dx[:], dt[:], Y[layer][:], ALU.mult).then_inc(dx_done, 1)

            def low_dt(x):
                dve.wait_ge(hi_done, 2 * x + 1)
                if not early(x, 1):
                    for half in s_in:
                        dve.wait_ge(half, 64 * x)
                nc.vector.tensor_tensor(dt_lo[:], dt[:], dt_hi[:].bitcast(f32), ALU.subtract).then_inc(dtlo_done, 1)

            def low_dx(x):
                dve.wait_ge(hi_done, 2 * x + 2)
                if not early(x, 1):
                    for half in s_in:
                        dve.wait_ge(half, 64 * x)
                nc.vector.tensor_tensor(dx_lo[:], dx[:], dx_hi[:].bitcast(f32), ALU.subtract).then_inc(dxlo_done, 1)


            def over_experts(a):
                return a.unsqueeze(2).to_broadcast(E3)

            def over_chunks(a):
                return a.unsqueeze(1).to_broadcast(E3)

            def route_norm(t):
                dve.wait_ge(r_rstd, t + 1)
                if not early(t, 1):
                    dve.wait_ge(r_trx, t)
                nc.vector.tensor_tensor(xn[:, 0:TOK], rcen[:], rrstd[:], ALU.mult).then_inc(r_xn, 1)

            def route_op(t, n, logits_in=POST, counts_in=POST):
                if n in LINKED:
                    dve.wait_ge(r_step, t * STEPS + LINKED[n])
                nv, fo = nc.vector, over_chunks(first_of[0:CHUNK, :])
                j, of = (0, prob) if n < 11 else (1, left)
                if n == 0:
                    dve.wait_ge(r_logit, t + 1)
                    lg = bank(logits_in, CHUNKS * EXPERTS, CHUNK).rearrange("p (k e) -> p k e", k=CHUNKS)
                    nv.tensor_tensor(prob[:], lg, over_chunks(brr[0:CHUNK, :]), ALU.add).then_inc(r_step, 1)
                elif n == 1:
                    nv.tensor_reduce(small_k[:], prob[:], AX.X, ALU.max).then_inc(r_step, 1)
                elif n == 2:
                    nv.tensor_tensor(prob[:], prob[:], over_experts(small_k[:]), ALU.subtract).then_inc(r_shift, 1)
                elif n == 3:
                    dve.wait_ge(r_pexp, t + 1)
                    nv.tensor_reduce(small_k[:], prob[:], AX.X, ALU.add).then_inc(r_step, 1)
                elif n == 4:
                    nv.reciprocal(small_k[:], small_k[:]).then_inc(r_step, 1)
                elif n == 5:
                    nv.tensor_tensor(prob[:], prob[:], over_experts(small_k[:]), ALU.mult).then_inc(r_step, 1)
                elif n in (6, 12):
                    nv.tensor_reduce(top[:, j, :], of[:], AX.X, ALU.max).then_inc(r_step, 1)
                elif n in (7, 13):
                    nv.tensor_tensor(same[:], of[:], over_experts(top[:, j, :]), ALU.is_equal).then_inc(r_step, 1)
                elif n in (8, 14):
                    nv.tensor_tensor(same[:], same[:], fo, ALU.mult).then_inc(r_step, 1)
                elif n in (9, 15):
                    nv.tensor_reduce(key[:], same[:], AX.X, ALU.max).then_inc(r_step, 1)
                elif n in (10, 16):
                    nv.tensor_tensor(hot[j][:], fo, over_experts(key[:]), ALU.is_equal).then_inc(r_step, 1)
                elif n == 11:
                    nv.scalar_tensor_tensor(out=left[:], in0=hot[0][:], scalar=-2.0, in1=prob[:], op0=ALU.mult,
                                            op1=ALU.add).then_inc(r_step, 1)
                elif n == 17:
                    nv.tensor_copy(gates[:, bass.ds(t, 1), :, :].rearrange("p t j k -> p (t j k)"),
                                   top[:].rearrange("p j k -> p (j k)"))
                    nv.tensor_tensor(same[:], hot[0][:], hot[1][:], ALU.add).then_inc(r_step, 1)
                elif n == 18:
                    if not early(t, 1):
                        dve.wait_ge(r_prefix, t)
                    nv.tensor_tensor(taken[:], same[:], over_experts(valid), ALU.mult).then_inc(r_mask, 1)
                elif n == 19:
                    dve.wait_ge(r_prefix, t + 1)
                    rank = bank(counts_in, CHUNKS * EXPERTS, CHUNK).rearrange("p (k e) -> p k e", k=CHUNKS)
                    nv.tensor_tensor(seat[:], rank, over_chunks(fill[0:CHUNK, :]), ALU.add).then_inc(r_step, 1)
                elif n == 20:
                    nv.tensor_tensor(fill[:], fill[:], bank(counts_in, 64 + EXPERTS)[:, 64:], ALU.add).then_inc(r_filled, 1)
                    for choice in range(TOP):
                        ins = nv.tensor_tensor((pick, same)[choice][:], hot[choice][:], seat[:], ALU.mult)
                    ins.then_inc(r_pick, 1)
                elif n == 21:
                    dve.wait_ge(r_pick, t + 1)
                    for choice in range(TOP):
                        ins = nv.tensor_reduce(seat_f[:, choice, :], (pick, same)[choice][:], AX.X, ALU.add)
                    ins.then_inc(r_sum, 1)
                elif n == 22:
                    if not early(t, 1):
                        dve.wait_ge(scattered, 128 * t)
                    dve.wait_ge(r_sum, t + 1)
                    nv.tensor_copy(staged[:, :, :, CHANNELS:ROW].bitcast(i32), plc[:].unsqueeze(3)).then_inc(r_places, 1)
                    nv.tensor_copy(seats[:], seat_f[:]).then_inc(r_seats, 1)
                elif n == 23:
                    dve.wait_ge(r_places, t + 1)
                    nv.tensor_scalar(plc[:], plc[:], float(CHUNKS * CHUNK), None, ALU.add).then_inc(r_moved, 1)

            LINKED = {1: 1, 2: 2, 4: 3, 5: 4}
            LINKED.update({n: n - 1 for n in range(6, 19)})
            LINKED[20] = 18
            OPS = 24
            STEPS = 18

            normal(0, None)
            step(0)
            step_times_y(0, 0)
            low_dt(0)
            low_dx(0)

            def slot(h, layer, after, project, embed, route=(None,) * 4):
                at = place(h, layer)
                par = parity_of(h, layer)

                def drive(i):
                    dve.wait_ge(rep_dx, 16 * h + i + 1)
                    nc.vector.tensor_tensor(bank(DX + (i + par) % 3), bank(DX + (i + par) % 3), B[par][:], ALU.mult).then_inc(b_done, 1)

                def chain(ops, t, i, half):
                    for n, where in ops.items():
                        if where == i + half / 2:
                            route_op(t, n)

                dve.wait_ge(b_ready, h + 1)
                drive(0)
                for i in range(GROUPS):
                    if i + 1 < GROUPS:
                        drive(i + 1)
                    if route[1] is not None:
                        chain(at["r_chain"], route[1], i, 0)
                    if route[3] is not None:
                        chain(at["r_seat_chain"], route[3], i, 0)
                    dve.wait_ge(exp_done, 16 * h + i + 1)
                    dve.wait_ge(b_done, 16 * h + i + 1)
                    if not (early(h, 1) and i < 4):
                        dve.wait_ge(hc_done, 16 * h + i - 3)
                    nc.vector.tensor_tensor_scan(state[i % 4][:], decay[i % 4][:].rearrange("p b t -> p (b t)"),
                                                 bank(DX + (i + par) % 3), 0.0, ALU.mult, ALU.add).then_inc(scan_done, 1)
                    if embed is not None and i == at["normal"]:
                        normal(embed, h)
                    if project:
                        x, l, _ = project
                        if i == at["dt"]:
                            step(x)
                        if i == at["dx"]:
                            step_times_y(x, l)
                        if i == at["dt_lo"]:
                            low_dt(x)
                        if i == at["dx_lo"]:
                            low_dx(x)
                    if route[1] is not None:
                        if i == at["r_xn"]:
                            route_norm(route[1])
                        chain(at["r_chain"], route[1], i, 1)
                    if route[3] is not None:
                        chain(at["r_seat_chain"], route[3], i, 1)

            run_slots(dve, slot)
            for n in range(19):
                route_op(TILES - 2, n)

            steps = [0]
            nblk, upto, start, here, tmp, used, ones = (a[:] for a in tab8)
            TABLE_OPS = 20

            def table_op(k, n):
                if k == 0 and n in (4, 10, 15, 16, 17):
                    return
                dve.wait_ge(t_step, steps[0])
                nv = nc.vector
                if n == 0:
                    ins = nv.tensor_tensor(nblk, fill[:], region, ALU.subtract)
                elif n == 1:
                    ins = nv.tensor_scalar(blocks_i[:], nblk, 127.0 * k, None, ALU.add)
                elif n == 2:
                    ins = nv.tensor_scalar(blocks_i[:], blocks_i[:], 7, None, ALU.logical_shift_right)
                elif n == 3:
                    ins = nv.tensor_copy(nblk, blocks_i[:])
                elif n == 4:
                    ins = nv.tensor_tensor(nblk, nblk, used, ALU.subtract)
                elif n == 5:
                    ins = nv.tensor_tensor_scan(upto, ones, nblk, float(EARLY * k), ALU.mult, ALU.add)
                elif n == 6:
                    ins = nv.tensor_tensor(start, upto, nblk, ALU.subtract)
                elif n == 7:
                    ins = nv.tensor_scalar(here, start, number, None, ALU.is_le)
                elif n == 8:
                    ins = nv.tensor_scalar(tmp, upto, number, None, ALU.is_gt)
                elif n == 9:
                    ins = nv.tensor_tensor(here, here, tmp, ALU.mult)
                elif n == 10:
                    ins = nv.tensor_tensor(start, start, used, ALU.subtract)
                elif n == 11:
                    ins = nv.tensor_scalar(tmp, start, number, -128.0, ALU.subtract, ALU.mult)
                elif n == 12:
                    ins = nv.tensor_tensor(tmp, tmp, region, ALU.add)
                elif n == 13:
                    ins = nv.tensor_tensor(tmp, tmp, here, ALU.mult)
                elif n == 14:
                    ins = nv.tensor_reduce(tab[:, 0:1], tmp, AX.X, ALU.add)
                elif n == 15:
                    ins = nv.tensor_scalar(tab[:, 2:3], upto[:, 7:8], number, None, ALU.is_le)
                elif n == 16:
                    ins = nv.tensor_tensor(tab[:, 2:3], tab[:, 2:3], spare, ALU.mult)
                elif n == 17:
                    ins = nv.tensor_tensor(tab[:, 0:1], tab[:, 0:1], tab[:, 2:3], ALU.add)
                elif n == 18:
                    ins = nv.tensor_tensor(tmp, here, expert, ALU.mult)
                else:
                    nv.tensor_reduce(tab[:, 1:2], tmp, AX.X, ALU.add).then_inc(t_cols, 1)
                    return
                ins.then_inc(t_step, 1)
                steps[0] += 1

            def set_table(k):
                a, b = ((0, EARLY), (EARLY, BLOCKS))[k]
                rows = bank((NSUM, PRE)[k], 2 * BLOCKS, 1).rearrange("a (c m) -> a c m", c=2)
                dve.wait_ge(t_rows, k + 1)
                nc.vector.tensor_copy(table[:, :, a:b], rows[:, :, a:b]).then_inc(t_ready, 1)

            nc.vector.memset(ones, 1.0).then_inc(t_step, 1)
            steps[0] += 1
            for n in range(TABLE_OPS):
                table_op(0, n)
            nc.vector.tensor_scalar(used, start, -1.0, float(EARLY), ALU.mult, ALU.add).then_inc(t_step, 1)
            steps[0] += 1
            dve.wait_ge(t_step, steps[0])
            nc.vector.scalar_tensor_tensor(out=used, in0=used, scalar=0.0, in1=nblk, op0=ALU.max, op1=ALU.min).then_inc(t_step, 1)
            steps[0] += 1
            for n in range(19, OPS):
                route_op(TILES - 2, n)
            set_table(0)

            dve.wait_ge(moe_in, 32)
            dve.wait_ge(t_ready, 1)

            def copy_down(e, b):
                nc.vector.tensor_copy(down_w[b][:], down_all[:, bass.ds(e, 1), :].rearrange("p e n -> p (e n)")).then_inc(down_copied, 1)

            def copy_goes(m, q, nth):
                dve.wait_ge(xg_in[q], 16 * nth)
                nc.vector.tensor_copy(goes[:, bass.ds(m, 1)], xg[q][:, CHANNELS:ROW].bitcast(i32)).then_inc(goes_ready, 1)

            def relus(b, n):
                dve.wait_ge(up_done, n)
                for f in (2, 3):
                    ins = nc.vector.tensor_scalar(hid[b][:, f, :], up_out(b, f),
                                                  up_w[b][:, HIDDEN + f:HIDDEN + f + 1], 0.0, ALU.add, ALU.max)
                ins.then_inc(relu_v, 1)

            def finish(b, n, before_):
                dve.wait_ge(down_done, n)
                if before_ is not None:
                    dve.wait_ge(stored[b], 16 * before_)
                nc.vector.tensor_tensor(ysb[b][:], bank(4 + b, 128), down_w[b][:, HIDDEN:DOWN],
                                        ALU.add).then_inc(y_ready, 1)

            def expert_of(m):
                return dve.value_load(table[0:1, 1, bass.ds(m, 1)], min_val=0, max_val=EXPERTS - 1)

            def turn(m, q, nth, done_before, is_last=False):
                b, o = q % 2, 1 - q % 2
                relus(b, m + 1)
                if done_before is not None:
                    finish(o, m, None if early(done_before, 1) else done_before)
                if not is_last:
                    e = expert_of(m + 1)
                    copy_goes(m + 1, (q + 1) % 4, nth)
                    if not early(m, 1):
                        dve.wait_ge(y_ready, m)
                    copy_down(e, o)

            copy_down(expert_of(0), 0)
            route_norm(TILES - 1)
            copy_goes(0, 0, 1)
            for n in range(3):
                route_op(TILES - 1, n, logits_in=NSUM)

            def beside(m):
                routing = {5: [18], 7: [19, 20, 21], 8: [22, 23], **{k: range(3 + 3 * k, 6 + 3 * k) for k in range(5)}}
                for n in routing.get(m, []):
                    route_op(TILES - 1, n, counts_in=PRE)
                if m == 8:
                    nc.vector.tensor_copy(ends[:], fill[:]).then_inc(pad_set, 1)
                if m >= 9:
                    for n in (2 * (m - 9), 2 * (m - 9) + 1):
                        if n < TABLE_OPS:
                            table_op(1, n)

            turn(0, 0, 1, None)
            beside(0)
            turn(1, 1, 1, 0)
            beside(1)
            turn(2, 2, 1, 0)
            beside(2)
            turn(3, 3, 2, 1)
            beside(3)

            def quad(j):
                for q in range(4):
                    turn(4 * j + q, q, j + 1 if q < 3 else j + 2, 2 * j + (-1, 0, 0, 1)[q])
                    if isinstance(j, int):
                        beside(4 * j + q)

            for j in range(1, 5):
                quad(j)
            set_table(1)
            with dve.Fori(5, BLOCKS // 4) as j:
                quad(j)
            turn(BLOCKS - 2, 0, BLOCKS // 4 + 1, BLOCKS // 2 - 2)
            turn(BLOCKS - 1, 1, None, BLOCKS // 2 - 1, is_last=True)
            finish(1, BLOCKS, BLOCKS // 2 - 1)

            for n, t in enumerate(DVE_TILES):
                dve.wait_ge(yb_in[t], 32)
                for choice in range(TOP):
                    if choice:
                        dve.wait_ge(half_sum, n + 1)
                    for k in range(CHUNKS):
                        before_ = yb[:, t, 0, k, :] if choice else htok[:, t, CHANNELS * k:CHANNELS * (k + 1)]
                        ins = nc.vector.scalar_tensor_tensor(out=yb[:, t, 0, k, :], in0=yb[:, t, choice, k, :],
                                                             scalar=gates[:, t, choice, k:k + 1], in1=before_,
                                                             op0=ALU.mult, op1=ALU.add)
                    ins.then_inc(summed if choice else half_sum, 1)

        @block.tensor
        def _(pe):
            pe.wait_ge(embed_in, 16 * 4)
            pe.wait_ge(tok_in, 32)
            pe.wait_ge(centre_set, 2)

            def tokens(t, prepared, k=PRE):
                if prepared is not None:
                    pe.wait_ge(c_ready, prepared)
                nc.tensor.matmul(bank(k), wtok[:], rows[:].rearrange("p b t -> p (b t)")[:, bass.ds(t * TOK, TOK)],
                                 start=True, stop=False)
                nc.tensor.matmul(bank(k), ident[:], pos2[:].rearrange("p b t -> p (b t)"), start=False,
                                 stop=True).then_inc(tok_done, 1)

            def centre(t, k=PRE):
                pe.wait_ge(h_done, t + 1)
                nc.tensor.matmul(bank(k), cen_w[:], tile_of(hT, t), start=True, stop=True).then_inc(cenm_done, 1)

            def variance(t, k=PRE):
                pe.wait_ge(sq_done, t + 1)
                nc.tensor.matmul(bank(k), mean_w[:], sq[:], start=True, stop=True).then_inc(var_done, 1)

            def project_dt(x, layer, ready, embed=None, staged_tiles=None):
                if staged_tiles is not None and not early(staged_tiles, 1):
                    pe.wait_ge(r_staged, 2 * staged_tiles)
                if layer == 0:
                    pe.wait_ge(y0_done, ready)
                else:
                    pe.wait_ge(linb_done, ready)
                if not early(x, 1):
                    pe.wait_ge(c_ready, x)
                if embed is not None:
                    pe.wait_ge(ln_done, embed + 1)
                nc.tensor.matmul(bank(PRE), wdt[:, layer, :], Y[layer][:], start=True, stop=True).then_inc(wdt_done, 1)

            def project_b(x, layer):
                pe.wait_ge(z_done, x + 1)
                nc.tensor.matmul(bank(PRE), wb[:, layer, :, :].rearrange("p n j -> p (n j)"), Y[layer][:],
                                 start=True, stop=True).then_inc(wb_done, 1)

            def project_c(x, layer):
                pe.wait_ge(b_ready, x + 1)
                nc.tensor.matmul(bank(PRE), wc[:, layer, :, :].rearrange("p n j -> p (n j)"), Y[layer][:],
                                 start=True, stop=True).then_inc(wc_done, 1)

            def linear(h, layer, logits_of=None, counts_of=None, k=POST):
                pe.wait_ge(relu_done, h + 1)
                if logits_of is not None:
                    pe.wait_ge(r_shift, logits_of + 1)
                if counts_of is not None:
                    pe.wait_ge(r_filled, counts_of + 1)
                nc.tensor.matmul(bank(k), wlin[:, layer, :], act_y[:], start=True, stop=True).then_inc(lin_done, 1)

            def decode(h, t, k=POST):
                pe.wait_ge(linb_done, h + 1)
                nc.tensor.matmul(bank(k), wdec[:], lin1[:], start=True, stop=False)
                nc.tensor.matmul(bank(k), ident[:], tile_of(hT, t), start=False, stop=True).then_inc(dec_done, 1)

            def skip_term(h, layer):
                if not early(h, 1):
                    pe.wait_ge(relu_done, h)
                for quad in range(4):
                    ins = nc.tensor.matmul(psum[32 * quad:32 * quad + 32, NSUM * BANK:NSUM * BANK + TOK],
                                           dskip[:, layer, 32 * quad:32 * quad + 32], Y[layer][:], start=True, stop=False)
                ins.then_inc(diag_done, 1)

            def sum_states(h, k):
                pe.wait_ge(hc_done, 16 * h + 4 * k + 4)
                for i in range(4 * k, 4 * k + 4):
                    quad = group(i) // 4
                    ins = nc.tensor.matmul(psum[32 * quad:32 * quad + 32, NSUM * BANK:NSUM * BANK + TOK],
                                           gath[:, group(i) % 4, :], hc[i % 8][:], start=False, stop=(k == 3))
                ins.then_inc(nsum_done, 1)

            def route_centre(t, k=POST):
                pe.wait_ge(resid_done, t + 1)
                nc.tensor.matmul(bank(k), cen_w[:], h_s[:, 0:TOK], start=True, stop=True).then_inc(r_cenm, 1)

            def route_variance(t, k=POST):
                pe.wait_ge(r_sq, t + 1)
                nc.tensor.matmul(bank(k), mean_w[:], rsq[:], start=True, stop=True).then_inc(r_var, 1)

            def route_logits(t, k=POST, free=None):
                pe.wait_ge(r_xn, t + 1)
                if free is not None:
                    pe.wait_ge(linb_done, free)
                for c in range(CHUNKS):
                    ins = nc.tensor.matmul(psum[0:CHUNK, k * BANK + EXPERTS * c:k * BANK + EXPERTS * (c + 1)],
                                           xn[:, CHUNK * c:CHUNK * (c + 1)], wr[:], start=True, stop=True)
                ins.then_inc(r_logit, 1)

            def turn_chunks(of, k):
                for c in range(CHUNKS):
                    ins = nc.tensor.transpose(psum[0:CHUNK, k * BANK + 128 * c:k * BANK + 128 * (c + 1)],
                                              of[:, CHUNK * c:CHUNK * (c + 1)], ident[:])
                return ins

            def route_turn_h(t, prepared=None, k=PRE):
                if prepared is not None:
                    pe.wait_ge(c_ready, prepared)
                turn_chunks(h_s, k).then_inc(r_trh, 1)

            def route_turn_x(t, prepared=None, k=PRE):
                pe.wait_ge(r_xn, t + 1)
                pe.wait_ge(r_htok, t + 1)
                if prepared is not None:
                    pe.wait_ge(c_ready, prepared)
                turn_chunks(xn, k).then_inc(r_trx, 1)

            def turn_table(k, at):
                pe.wait_ge(t_cols, k + 1)
                for c in range(2):
                    ins = nc.tensor.matmul(psum[0:1, at * BANK + c * BLOCKS:at * BANK + (c + 1) * BLOCKS], tab[0:BLOCKS, c:c + 1],
                                           ident[0:BLOCKS, 0:BLOCKS], start=True, stop=True)
                ins.then_inc(t_rows, 1)

            def route_prefix(t, k=POST):
                pe.wait_ge(r_mask, t + 1)
                at0 = k * BANK
                for c in range(CHUNKS):
                    dst = psum[0:CHUNK, at0 + EXPERTS * c:at0 + EXPERTS * (c + 1)]
                    for q in range(c):
                        nc.tensor.matmul(dst, onesb[:, 0:CHUNK], taken[:, q, :], start=(q == 0), stop=False)
                    nc.tensor.matmul(dst, beforeb[:], taken[:, c, :], start=(c == 0), stop=True)
                for q in range(CHUNKS):
                    ins = nc.tensor.matmul(psum[:, at0 + 64:at0 + 64 + EXPERTS], onesb[:], taken[:, q, :], start=(q == 0),
                                           stop=(q == CHUNKS - 1))
                ins.then_inc(r_prefix, 1)

            tokens(0, None)
            centre(0)
            tokens(1, None, POST)
            variance(0)
            centre(1, POST)
            pe.wait_ge(param_in, 16 * PARAM_DMAS)
            pe.wait_ge(consts, CONSTS)
            project_dt(0, 0, 1)
            project_b(0, 0)
            variance(1, POST)
            project_c(0, 0)

            def slot(h, layer, after, project, embed, route=(None,) * 4):
                at = place(h, layer)
                par = parity_of(h, layer)
                pe.wait_ge(s_in[0], 64 * (h + 1))
                for i in range(GROUPS):
                    g = group(i)
                    if i == 2:
                        pe.wait_ge(s_in[1], 64 * (h + 1))
                    if not (early(h, 1) and i < 2):
                        pe.wait_ge(exp_done, 16 * h + i - 1)
                    nc.tensor.matmul(bank(DT + i % 2), spreadr[:, g % 8, :], S_dt[par][:, g // 8, :], start=True,
                                     stop=True).then_inc(rep_dt, 1)
                    if not (early(h, 1) and i < 3):
                        pe.wait_ge(scan_done, 16 * h + (i - 2 if i >= 3 else ((-1, 0, -2), (-2, -1, 0))[par][i]))
                    nc.tensor.matmul(bank(DX + (i + par) % 3), spreadr[:, g % 8, :], S_dx[par][:, g // 8, :], start=True,
                                     stop=True).then_inc(rep_dx, 1)
                    if after and i in (at["sum2"], at["sum3"]):
                        sum_states(h - 1, 2 if i == at["sum2"] else 3)
                    if i == at["diag"]:
                        skip_term(h, layer)
                    if after:
                        t, l = after
                        if i == at["lin"]:
                            linear(h - 1, l, route[1] if (at["r_logit"] or GROUPS) < i else None, route[3])
                        if i == at["dec"] and l == 1:
                            decode(h - 1, t)
                    if i in (at["sum0"], at["sum1"]):
                        sum_states(h, 0 if i == at["sum0"] else 1)
                    if route[0] is not None and i == at["r_cenm"]:
                        route_centre(route[0])
                    if route[1] is not None:
                        t = route[1]
                        if i == at["r_var"]:
                            route_variance(t)
                        if i == at["r_logit"]:
                            route_logits(t, free=h if isinstance(h, int) and h == SLOTS - 2 else None)
                        if i == at["r_trh"]:
                            route_turn_h(t, (h + 1 if i < at["wdt"] else h + 2) if project else None)
                        if i == at["r_trx"]:
                            route_turn_x(t, h + 2)
                    if route[3] is not None and i == at["r_prefix"]:
                        route_prefix(route[3])
                    if embed is not None:
                        if i == at["tok"]:
                            tokens(embed, (h + 1 if at["tok"] < at["wdt"] else h + 2))
                        if i == at["cenm"]:
                            centre(embed)
                        if i == at["var"]:
                            variance(embed)
                    if project:
                        x, l, ready = project
                        if i == at["wdt"]:
                            if route[1] is not None and at["r_htok"] < i:
                                pe.wait_ge(r_htok, route[1] + 1)
                            project_dt(x, l, ready, embed if embed is not None and at["lnv"] is not None and at["lnv"] < i else None,
                                       route[0])

                        if i == at["wb"]:
                            project_b(x, l)
                        if i == at["wc"]:
                            project_c(x, l)

            run_slots(pe, slot)
            route_logits(TILES - 2)
            route_turn_x(TILES - 2)
            sum_states(SLOTS - 1, 2)
            sum_states(SLOTS - 1, 3)
            linear(SLOTS - 1, 1, k=0)
            route_prefix(TILES - 2)
            decode(SLOTS - 1, TILES - 1, k=1)
            turn_table(0, NSUM)
            route_centre(TILES - 1, k=2)

            def turn_x(q, nth, m):
                pe.wait_ge(xg_in[q], 16 * nth)
                nc.tensor.transpose(bank(POST, 128), xg[q][:, 0:CHANNELS], ident[:]).then_inc(turned, 1)

            def up(b, m):
                pe.wait_ge(xT_ready, m + 1)
                pe.wait_ge(up_copied, m + 1)
                for f in range(FCH):
                    ins = nc.tensor.matmul(up_out(b, f),
                                           up_w[b][:, 128 * f:128 * (f + 1)], xT[b][:], start=True, stop=True)
                ins.then_inc(up_done, 1)

            def down(b, m):
                pe.wait_ge(relu_a, m + 1)
                pe.wait_ge(relu_v, m + 1)
                pe.wait_ge(down_copied, m + 1)
                for f in range(FCH):
                    ins = nc.tensor.matmul(bank(4 + b, 128), hid[b][:, f, :],
                                           down_w[b][:, 128 * f:128 * (f + 1)], start=(f == 0), stop=(f == FCH - 1))
                ins.then_inc(down_done, 1)

            pe.wait_ge(r_filled, TILES - 1)
            turn_x(0, 1, 0)
            route_variance(TILES - 1, k=3)
            up(0, 0)
            route_logits(TILES - 1, k=NSUM)
            turn_x(1, 1, 1)
            route_turn_h(TILES - 1, k=PRE)

            def turn(m, q, nth):
                up(q % 2, m)
                if nth is not None:
                    turn_x((q + 1) % 4, nth, m + 1)
                down(1 - q % 2, m - 1)

            turn(1, 1, 1)
            route_turn_x(TILES - 1, k=PRE)
            pe.wait_ge(r_shift, TILES)
            turn(2, 2, 1)
            turn(3, 3, 2)

            def quad(j):
                for q in range(4):
                    turn(4 * j + q, q, j + 1 if q < 3 else j + 2)

            for m in (4, 5, 6):
                turn(m, m % 4, 2)
            pe.wait_ge(r_staged, 2 * TILES)
            route_prefix(TILES - 1, k=PRE)
            turn(7, 3, 3)
            with pe.Fori(2, 5) as j:
                quad(j)
            turn_table(1, PRE)
            with pe.Fori(5, BLOCKS // 4) as j:
                quad(j)
            turn(BLOCKS - 2, 0, BLOCKS // 4 + 1)
            turn(BLOCKS - 1, 1, None)
            down(1, BLOCKS - 1)


def kernel(**inputs):
    import concourse.bacc as bacc
    from concourse.bass_utils import run_bass_kernel_spmd

    g = {k: np.asarray(v) for k, v in inputs.items()}
    c = np.ascontiguousarray
    at = lambda n: g["L0_attn_" + n]
    fn = lambda n: g["L0_ffn_" + n]
    samples = (LENGTH + 1) * STRIDE
    cols = [at("bdt").T, np.repeat(at("bB"), GCH, axis=1).T, np.repeat(at("bC"), GCH, axis=1).T, at("D_skip").T, at("blin").T,
            at("bdec")[:, None], np.full((128, 1), EPS, np.float32), np.zeros((128, 1), np.float32), np.ones((128, 1), np.float32)]
    p = np.arange(128)
    spread = np.zeros((128, 8, 128), np.float32)
    gather = np.zeros((128, 4, 32), np.float32)
    for r in range(8):
        spread[:, r, :] = (p[:, None] % 64) == 8 * r + p[None, :] % 8
    for r in range(4):
        gather[:, r, :] = p[None, :32] == 8 * r + p[:, None] % 8
    before = np.triu(np.ones((CHUNK, CHUNK), np.float32), 1)
    small = np.zeros((128, 6 * EXPERTS), np.float32)
    small[:, 0:8] = EXPERTS - np.arange(EXPERTS)
    small[:, 8:16] = CAP * np.arange(EXPERTS)
    small[:, 16:20] = p[:, None] < np.array(CHUNK_TOK)
    small[:, 20] = p
    small[:, 21] = SPARE + 128 * np.maximum(p - FEWEST, 0)
    small[:, 24:32] = np.arange(EXPERTS)
    places = (RESULT * np.arange(TOP)[:, None] + CHUNK * np.arange(CHUNKS)[None, :])[None] + p[:CHUNK, None, None]
    arrays = {
        "x_rows": g["x"][:, :samples, 0].reshape(SEQS, LENGTH + 1, STRIDE).transpose(2, 0, 1),
        "w_tok": g["L0_tok_W"].T,
        "pos": g["L0_tok_pos_embed"][0, :LENGTH].T,
        "a_cols": at("A").reshape(LAYERS, GROUPS, GCH, STATES).transpose(3, 2, 0, 1).reshape(128, LAYERS, GROUPS),
        "w_dt": at("Wdt").transpose(1, 0, 2), "w_b": at("WB").transpose(1, 0, 2), "w_c": at("WC").transpose(1, 0, 2),
        "w_lin": at("Wlin").transpose(1, 0, 2), "w_dec": at("Wdec"),
        "vecs": np.concatenate(cols, axis=1),
        "w_r": fn("Wr"), "b_r": np.broadcast_to(fn("br"), (128, EXPERTS)),
        "w_up": np.concatenate([fn("W1").transpose(1, 0, 2), fn("b1").reshape(EXPERTS, FCH, 128).transpose(2, 0, 1)], axis=2),
        "w_down": np.concatenate([fn("W2").reshape(EXPERTS, FCH, 128, 128).transpose(2, 0, 1, 3).reshape(128, EXPERTS, HIDDEN),
                                  np.broadcast_to(fn("b2"), (128, EXPERTS, CHANNELS))], axis=2),
        "spread": spread, "gather": gather, "eye": np.eye(128, dtype=np.float32), "before": before,
        "small": small, "places": places.astype(np.float32),
    }
    arrays = {k: c(v) for k, v in arrays.items()}
    nc = bacc.Bacc("TRN2", target_bir_lowering=False, num_devices=1)
    args = [nc.dram_tensor(k, v.shape, mybir.dt.from_np(v.dtype), kind="ExternalInput").ap() for k, v in arrays.items()]
    out = nc.dram_tensor("out", (TOKENS, CHANNELS), mybir.dt.float32, kind="ExternalOutput").ap()
    audio_tower(nc, *args, out)
    r = run_bass_kernel_spmd(nc, [arrays], core_ids=[0])
    return r.results[0]["out"].reshape(SEQS, LENGTH, CHANNELS)
```
